# Optimizing a Trainium2 kernel written in Bass

```python
import numpy as np
import jax
import jax.numpy as jnp

def _softmax(x, axis=-1):
    return jax.nn.softmax(x, axis=axis)

def _gelu(x):
    return jax.nn.gelu(x, approximate=True)

def _silu(x):
    return jax.nn.silu(x)

def _sigmoid(x):
    return jax.nn.sigmoid(x)

def _layernorm(x, axis=-1, eps=1e-05):
    m = jnp.mean(x, axis=axis, keepdims=True)
    v = jnp.var(x, axis=axis, keepdims=True)
    return (x - m) / jnp.sqrt(v + eps)

def _scatter_add(tgt, idx, src, axis=0):
    return tgt.at[idx].add(src)

def _segment_sum(src, seg, n):
    return jax.ops.segment_sum(src, seg, n)
kernel_name = 'mk_cond_resid_d2_seqx_r2_0c5fbf'

def setup_inputs(seed: int=0):
    np.random.seed(seed)
    _w = jnp.asarray

    def _rec_inputs():
        import jax
        import jax.numpy as jnp
        _rk = jax.random.key(seed)
        x = 0.0001734 + 0.8201 * jax.random.normal(jax.random.fold_in(_rk, 1), (32, 128, 2048), jnp.float32)
        _lenS = 128 - jax.random.randint(jax.random.fold_in(_rk, 7), (32,), 0, max(1, 128 // 4) + 1, jnp.int32)
        _lenS2 = 128 - jax.random.randint(jax.random.fold_in(_rk, 8), (32,), 0, max(1, 128 // 4) + 1, jnp.int32)
        itok_B_0_7 = jax.random.randint(jax.random.fold_in(_rk, 11), (32,), 0, 8, jnp.int32)
        itok_B_2182_4065 = jax.random.randint(jax.random.fold_in(_rk, 13), (32,), 1091, 2033, jnp.int32)
        itok_B_78_3631 = jax.random.randint(jax.random.fold_in(_rk, 14), (32,), 78, 1816, jnp.int32)
        return (x, itok_B_0_7, itok_B_2182_4065, itok_B_78_3631, _lenS)
    x, itok_B_0_7, itok_B_2182_4065, itok_B_78_3631, _lenS = _rec_inputs()

    def _L0_cond_setup():
        import jax, jax.numpy as jnp
        import numpy as np
        SESSION_CHANNELS = [128, 160, 192, 224, 240, 248, 252, 128]
        N_SESS = len(SESSION_CHANNELS)
        B, MAX_C, MAX_T = (16, 128, 2048)
        HID, N_SRC = (256, 128)
        key = jax.random.key(seed)
        ks = jax.random.split(key, 7)
        session_ids = jax.random.randint(ks[0], (B,), 0, N_SESS)
        chan_table = jnp.asarray(SESSION_CHANNELS)
        channel_counts = chan_table[session_ids]
        seq_lens = jax.random.randint(ks[1], (B,), MAX_T // 2, MAX_T + 1)
        x = jax.random.normal(ks[2], (B, MAX_C, MAX_T), jnp.float32)
        cmask = (jnp.arange(MAX_C)[None, :] < channel_counts[:, None]).astype(x.dtype)
        tmask = (jnp.arange(MAX_T)[None, :] < seq_lens[:, None]).astype(x.dtype)
        x = x * cmask[:, :, None] * tmask[:, None, :]
        lim1 = 1.0 / np.sqrt(MAX_C)
        W_sess = jax.random.uniform(ks[3], (N_SESS, MAX_C, HID), jnp.float32, -lim1, lim1)
        b_sess = jax.random.uniform(ks[4], (N_SESS, HID), jnp.float32, -lim1, lim1)
        lim2 = 1.0 / np.sqrt(HID)
        W2 = jax.random.uniform(ks[5], (HID, N_SRC), jnp.float32, -lim2, lim2)
        b2 = jax.random.uniform(ks[6], (N_SRC,), jnp.float32, -lim2, lim2)
        return dict(x=x, session_ids=session_ids, channel_counts=channel_counts, seq_lens=seq_lens, W_sess=W_sess, b_sess=b_sess, W2=W2, b2=b2)
    _L0_cond_all = _L0_cond_setup()
    _L0_cond_in = {k: v for k, v in _L0_cond_all.items() if k in ('W_sess', 'b_sess', 'W2', 'b2')}
    del _L0_cond_all

    def _L1_cond_setup():
        import math
        import jax, jax.numpy as jnp
        import numpy as np
        B, H, N, L = (16, 128, 64, 2048)
        DT_MIN, DT_MAX = (0.001, 0.1)

        def _get_kernel(log_dt, C, log_A_real, A_imag, length):
            dt = jnp.exp(log_dt)
            Cc = C[..., 0] + 1j * C[..., 1]
            A = -jnp.exp(log_A_real) + 1j * A_imag
            dtA = A * dt[:, None]
            Ct = Cc * (jnp.exp(dtA) - 1.0) / A
            P = dtA[:, :, None] * jnp.arange(length, dtype=jnp.float32)
            K = 2.0 * jnp.einsum('hn,hnl->hl', Ct, jnp.exp(P)).real
            return K
        key = jax.random.key(seed)
        ks = jax.random.split(key, 5)
        u = jax.random.normal(ks[0], (B, H, L), dtype=jnp.float32)
        log_dt = jax.random.uniform(ks[1], (H,), dtype=jnp.float32) * (math.log(DT_MAX) - math.log(DT_MIN)) + math.log(DT_MIN)
        C = jax.random.normal(ks[2], (H, N, 2), dtype=jnp.float32)
        log_A_real = jnp.log(0.5 * jnp.ones((H, N), dtype=jnp.float32))
        A_imag = math.pi * jnp.broadcast_to(jnp.arange(N, dtype=jnp.float32), (H, N))
        D = jax.random.normal(ks[3], (H,), dtype=jnp.float32)
        length = jax.random.randint(ks[4], (B,), 1, L + 1, dtype=jnp.int32)
        return {'u': u, 'log_dt': log_dt, 'C': C, 'log_A_real': log_A_real, 'A_imag': A_imag, 'D': D, 'length': length}
    _L1_cond_all = _L1_cond_setup()
    _L1_cond_in = {k: v for k, v in _L1_cond_all.items() if k in ('log_dt', 'C', 'log_A_real', 'A_imag', 'D')}
    del _L1_cond_all
    return {'x': x, 'itok_B_0_7': itok_B_0_7, 'itok_B_2182_4065': itok_B_2182_4065, 'itok_B_78_3631': itok_B_78_3631, '_lenS': _lenS, 'L0_cond_W_sess': _L0_cond_in['W_sess'], 'L0_cond_b_sess': _L0_cond_in['b_sess'], 'L0_cond_W2': _L0_cond_in['W2'], 'L0_cond_b2': _L0_cond_in['b2'], 'L1_cond_log_dt': _L1_cond_in['log_dt'], 'L1_cond_C': _L1_cond_in['C'], 'L1_cond_log_A_real': _L1_cond_in['log_A_real'], 'L1_cond_A_imag': _L1_cond_in['A_imag'], 'L1_cond_D': _L1_cond_in['D']}

def reference(x, itok_B_0_7, itok_B_2182_4065, itok_B_78_3631, _lenS, L0_cond_W_sess, L0_cond_b_sess, L0_cond_W2, L0_cond_b2, L1_cond_log_dt, L1_cond_C, L1_cond_log_A_real, L1_cond_A_imag, L1_cond_D):
    import jax
    import jax.numpy as jnp

    def _L0_cond_ref(x, session_ids, channel_counts, seq_lens, W_sess, b_sess, W2, b2):
        import jax, jax.numpy as jnp
        import numpy as np
        SESSION_CHANNELS = [128, 160, 192, 224, 240, 248, 252, 128]
        N_SESS = len(SESSION_CHANNELS)
        B, MAX_C, MAX_T = (16, 128, 2048)
        HID, N_SRC = (256, 128)
        cmask = (jnp.arange(x.shape[1])[None, :] < channel_counts[:, None]).astype(x.dtype)
        xm = x * cmask[:, :, None]
        W = W_sess[session_ids]
        b = b_sess[session_ids]
        h = jnp.einsum('bct,bch->bht', xm, W) + b[:, :, None]
        h = jax.nn.gelu(h, approximate=False)
        out = jnp.einsum('bht,hs->bst', h, W2) + b2[None, :, None]
        tmask = (jnp.arange(x.shape[2])[None, :] < seq_lens[:, None]).astype(x.dtype)
        return out * tmask[:, None, :]

    def _L1_cond_ref(u, log_dt, C, log_A_real, A_imag, D, length):
        import math
        import jax, jax.numpy as jnp
        import numpy as np
        B, H, N, L = (16, 128, 64, 2048)
        DT_MIN, DT_MAX = (0.001, 0.1)

        def _get_kernel(log_dt, C, log_A_real, A_imag, length):
            dt = jnp.exp(log_dt)
            Cc = C[..., 0] + 1j * C[..., 1]
            A = -jnp.exp(log_A_real) + 1j * A_imag
            dtA = A * dt[:, None]
            Ct = Cc * (jnp.exp(dtA) - 1.0) / A
            P = dtA[:, :, None] * jnp.arange(length, dtype=jnp.float32)
            K = 2.0 * jnp.einsum('hn,hnl->hl', Ct, jnp.exp(P)).real
            return K
        Bq, Hq, Lq = u.shape
        K = _get_kernel(log_dt, C, log_A_real, A_imag, Lq)
        n = 2 * Lq
        kf = jnp.fft.rfft(K, n=n)
        uf = jnp.fft.rfft(u, n=n)
        y = jnp.fft.irfft(uf * kf[None], n=n)[..., :Lq]
        y = y + u * D[:, None]
        mask = (jnp.arange(Lq)[None, :] < length[:, None]).astype(u.dtype)
        return y * mask[:, None, :]
    x = x + _L0_cond_ref(x, itok_B_0_7, _lenS, itok_B_2182_4065, L0_cond_W_sess, L0_cond_b_sess, L0_cond_W2, L0_cond_b2)
    x = x + _L1_cond_ref(x, L1_cond_log_dt, L1_cond_C, L1_cond_log_A_real, L1_cond_A_imag, L1_cond_D, itok_B_78_3631)
    return x

_drawn_inputs = setup_inputs


def setup_inputs(seed=0):
    import zlib

    import numpy as np

    out = dict(_drawn_inputs(seed))
    spreads = {'L1_cond_log_A_real': (-0.6931471824645996, 0.2)}
    factors = {}
    for name, (base, spread) in spreads.items():
        noise = np.random.default_rng([zlib.crc32(name.encode()), seed]).standard_normal(out[name].shape)
        drawn = base * np.exp(spread * noise) if base else spread * noise
        out[name] = jnp.asarray(drawn.astype(out[name].dtype))
    for name, factor in factors.items():
        out[name] = (out[name] * factor).astype(out[name].dtype)
    return out
```

```python
import math
from contextlib import ExitStack

import concourse.bass as bass
from concourse import mybir

F32 = mybir.dt.float32
BF16 = mybir.dt.bfloat16
I32 = mybir.dt.int32
ACT = mybir.ActivationFunctionType
ALU = mybir.AluOpType

P = 128
B, CH, L = 32, 128, 2048
HID, SESS, MODES = 256, 8, 64
T = 128
SUP = 2 * T
NSUP = L // SUP
BLK = 512
NBLK = L // BLK
KPAD = 3 * T

LOG2E = math.log2(math.e)
LN2_HI = 0.693359375
LN2_LO = math.log(2.0) - LN2_HI
ROUND = 1.5 * 2.0 ** 23
TWO_PI = 6.283185


def session_and_state_space_layer(nc, x, sid, seq_len, out_len, chan_count, w_sess, b_sess, w2, b2,
                                  log_dt, c_in, log_a, a_imag, d_in, out):
    ctx = ExitStack()
    with ctx:
        def sb(name, shape, dt=F32):
            return ctx.enter_context(nc.sbuf_tensor(name, shape, dt))

        def sem(name):
            return ctx.enter_context(nc.semaphore(name))

        def pair(name, shape, dt=F32, n=2):
            return [sb(f"{name}{i}", shape, dt) for i in range(n)]

        mid_dram = nc.dram_tensor("mid_scratch", [NSUP, B, CH, SUP], F32, kind="Internal").ap()
        kpad_dram = nc.dram_tensor("kernel_scratch", [CH, KPAD], F32, kind="Internal").ap()

        expin = sb("expin", [P, MODES + 1])
        aim = sb("aim", [P, MODES])
        cc2 = sb("cc2", [P, MODES, 2])
        d_row = sb("d_row", [1, CH])
        w2_raw = sb("w2_raw", [P, 2, CH])
        b2_col = sb("b2_col", [P, 1])
        bs_raw = sb("bs_raw", [SESS, HID])
        sid8 = sb("sid8", [SESS, B], I32)
        cc_i = sb("cc_i", [P, B], I32)
        len_i = sb("len_i", [P, B], I32)
        olen_i = sb("olen_i", [P, 1], I32)
        sid_row = sb("sid_row", [1, B], I32)

        ident = sb("ident", [P, P])
        swap = sb("swap", [P, P])
        part = sb("part", [P, 1])
        time_row = sb("time_row", [P, L])
        idx_b = sb("idx_b", [P, 16])
        idx_a = sb("idx_a", [P, 16])
        sgn = sb("sgn", [P, 1])
        zeros = sb("zeros", [P, T])

        onehot = sb("onehot", [SESS, B])
        ccf = sb("ccf", [P, B])
        cmask = sb("cmask", [P, B])
        lenf = sb("lenf", [P, B])
        bias = sb("bias", [P, B, 2])
        w2hi = sb("w2hi", [P, 2, CH], BF16)
        w2lo = sb("w2lo", [P, 2, CH], BF16)

        ex = [sb(f"ex{i}", [P, MODES + 1]) for i in range(4)]
        ex_i = sb("ex_i", [P, MODES + 1], I32)
        hv = [sb(f"hv{i}", [P, MODES]) for i in range(12)]
        par = sb("par", [P, 4, 2, MODES])
        par_t = sb("par_t", [P, 4, CH])
        q_cos = sb("q_cos", [P, CH, 16])
        q_sin = sb("q_sin", [P, CH, 16])
        l_re = sb("l_re", [P, CH, 16])
        l_im = sb("l_im", [P, CH, 16])
        z1 = sb("z1", [P, CH, 16])
        z2 = sb("z2", [P, CH, 16])
        x1 = sb("x1", [P, CH, 16])
        x2 = sb("x2", [P, CH, 16])
        r_diag = sb("r_diag", [P, CH])
        r_off = sb("r_off", [P, CH])
        rv = [sb(f"rv{i}", [P, CH]) for i in range(3)]
        thr = sb("thr", [P, 2])
        omask = sb("omask", [P, 2, SUP])

        x_in = pair("x_in", [P, L])
        mid_out = pair("mid_out", [P, L])
        x_hi = sb("x_hi", [P, 4, BLK], BF16)
        x_lo = sb("x_lo", [P, 4, BLK], BF16)
        w_raw = pair("w_raw", [P, HID])
        w_m = sb("w_m", [P, HID])
        w_hi = pair("w_hi", [P, HID], BF16)
        w_lo = pair("w_lo", [P, HID], BF16)
        len_col = pair("len_col", [P, 1])
        bias_col = pair("bias_col", [P, 2])
        g32 = sb("g32", [P, 2, 2, BLK])
        g_hi = pair("g_hi", [P, 2, BLK], BF16)
        g_lo = pair("g_lo", [P, 2, BLK], BF16)
        tmask = pair("tmask", [P, BLK])
        mid_m = pair("mid_m", [P, BLK])

        SLOTS, GH = 4, 2
        xt = [x_in[s // 2][:, s % 2 * 1024:s % 2 * 1024 + 1024].rearrange(
            "p (a g t) -> p a g t", a=2, g=GH) for s in range(SLOTS)]
        toep = [mid_out[0][:, s * 512:s * 512 + 512].rearrange("p (g t) -> p g t", g=GH)
                for s in range(SLOTS)]
        u_sb = [g32[:, 0, k, :].rearrange("p (c t) -> p c t", c=2) for k in range(2)]
        b_sb = pair("b_sb", [P, 2, P])
        s_sb = pair("s_sb", [P, SUP])
        c_sb = pair("c_sb", [P, 16, 16])
        e_sb = pair("e_sb", [P, 16, 16])
        r_sb = pair("r_sb", [P, P])
        ctmp = pair("ctmp", [P, 16, 16])
        etmp = pair("etmp", [P, 16, 16])
        y_m = [g32[:, 1, k, :].rearrange("p (a t) -> p a t", a=2) for k in range(2)]
        o_sb = [mid_out[1][:, k * 512:(k + 1) * 512].rearrange("p (a t) -> p a t", a=2) for k in range(2)]

        bank = [ctx.enter_context(nc.psum_tensor(f"bank{i}", [P, 512], F32)) for i in range(8)]
        hid_ps = [[bank[2 * i + h] for h in range(2)] for i in range(2)]
        mid_ps = [bank[4], bank[5]]
        up_ps = [bank[0], bank[1]]
        v_ps = [bank[2], bank[3]]
        y_ps = [bank[4], bank[5]]
        bt_ps = bank[6]

        params_in = sem("params_in")
        sid_in = sem("sid_in")
        consts = sem("consts")
        pool_passed = sem("pool_passed")
        pool_step = sem("pool_step")
        dve_step = sem("dve_step")
        waves_in = sem("waves_in")
        waves = sem("waves")
        to_pe = sem("to_pe")
        pe_setup = sem("pe_setup")
        z_ready = sem("z_ready")
        tables_ready = sem("tables_ready")
        kernel_ready = sem("kernel_ready")
        kpad_out = sem("kpad_out")
        x_loaded = [sem(f"x_loaded{i}") for i in range(2)]
        w_loaded = [sem(f"w_loaded{i}") for i in range(2)]
        w_step = sem("w_step")
        w_ready = sem("w_ready")
        x_high = sem("x_high")
        x_split = sem("x_split")
        mask_ready = sem("mask_ready")
        hid_ready = sem("hid_ready")
        gelu_done = sem("gelu_done")
        g_high = sem("g_high")
        g_low = sem("g_low")
        mid_ready = sem("mid_ready")
        mid_masked = sem("mid_masked")
        mid_added = sem("mid_added")
        mid_stored = [sem(f"mid_stored{i}") for i in range(2)]
        xt_loaded = [sem(f"xt_loaded{i}") for i in range(SLOTS)]
        toep_loaded = [sem(f"toep_loaded{i}") for i in range(SLOTS)]
        u_turned = sem("u_turned")
        b_turned = sem("b_turned")
        u_ready = sem("u_ready")
        b_ready = sem("b_ready")
        e_step = sem("e_step")
        e_ready = sem("e_ready")
        c_step = sem("c_step")
        c_ready = sem("c_ready")
        r_step = sem("r_step")
        r_ready = sem("r_ready")
        v_done = sem("v_done")
        state_added = sem("state_added")
        state_ready = sem("state_ready")
        y_local = sem("y_local")
        y_done = sem("y_done")
        y_masked = sem("y_masked")
        o_ready = sem("o_ready")
        o_stored = [sem(f"o_stored{i}") for i in range(2)]

        block = ctx.enter_context(nc.Block())

        def wait(eng, s, value):
            if not isinstance(value, int) or value > 0:
                eng.wait_ge(s, value)

        def wait_apart(eng, s, value):
            wait(eng, s, value)
            eng.sem_inc(pool_passed, 1)

        def peeled(eng, count, body):
            body(0, True, False)
            with eng.Fori(1, count - 1) as i:
                body(i, False, False)
            body(count - 1, False, True)

        def bcast(row, n):
            return row.unsqueeze(1).to_broadcast([P, n, row.shape[-1]])

        def outer(col, n):
            return col.unsqueeze(2).to_broadcast([P, col.shape[-1], n])

        def row_outer(table, h):
            return table[:, bass.ds(h, 1), :].rearrange("p a r -> p (a r)").unsqueeze(2).to_broadcast([P, 16, 16])

        def row_bcast(table, h):
            return table[:, bass.ds(h, 1), :].to_broadcast([P, 16, 16])

        BPI = 2
        NI1 = B // BPI
        HPI = SLOTS * GH
        NI2 = CH // HPI
        KA = 1024 // SUP

        @block.sync
        def _(sp):
            sp.dma_start(sid_row[:, :], sid.rearrange("(a n) -> a n", a=1)).then_inc(sid_in, 16)
            for dst, src in (
                (expin[:, 0:MODES], log_a), (expin[:, MODES:MODES + 1], log_dt.rearrange("(p a) -> p a", a=1)),
                (aim[:, :], a_imag), (cc2[:, :, :], c_in), (d_row[:, :], d_in.rearrange("(a n) -> a n", a=1)),
                (w2_raw[:, :, :], w2.rearrange("(a p) s -> p a s", p=P)),
                (b2_col[:, :], b2.rearrange("(p a) -> p a", a=1)), (bs_raw[:, :], b_sess),
                (sid8[:, :], sid.partition_broadcast(SESS)), (cc_i[:, :], chan_count.partition_broadcast(P)),
                (len_i[:, :], seq_len.partition_broadcast(P)),
            ):
                sp.dma_start(dst, src).then_inc(params_in, 16)
            for k in range(KA):
                sp.dma_start(olen_i[k * B:(k + 1) * B, :],
                             out_len.rearrange("(p a) -> p a", a=1)).then_inc(params_in, 16)

            sp.wait_ge(sid_in, 16)

            def load_batch(b, s):
                sp.dma_start(x_in[s][:, :], x[bass.ds(b, 1), :, :].rearrange("a c t -> (a c) t")
                             ).then_inc(x_loaded[s], 16)
                session = sp.value_load(sid_row[0:1, bass.ds(b, 1)], min_val=0, max_val=SESS - 1)
                sp.dma_start(w_raw[s][:, :], w_sess[bass.ds(session, 1), :, :].rearrange("a c h -> (a c) h")
                             ).then_inc(w_loaded[s], 16)

            load_batch(0, 0)
            load_batch(1, 1)

            def store_batches(i, first, last):
                for s in range(BPI):
                    b = i * BPI + s
                    sp.wait_ge(mid_added, NBLK * b + NBLK)
                    sp.dma_start(mid_dram[:, bass.ds(b, 1), :, :].rearrange("k a c t -> c (k a) t"),
                                 mid_out[s][:, :].rearrange("c (k t) -> c k t", t=SUP)).then_inc(mid_stored[s], 16)
                    if not last:
                        load_batch(b + BPI, s)
            peeled(sp, NI1, store_batches)
            for s in range(BPI):
                sp.wait_ge(mid_stored[s], 16 * NI1)
            sp.wait_ge(kpad_out, 32)

            def load_group(g, s):
                for a in range(2):
                    src = bass.AP(tensor=mid_dram.tensor, offset=0,
                                  ap=[[CH * SUP, NSUP * B], [SUP, CH], [1, SUP]])
                    sp.dma_start(xt[s][:, a, :, :],
                                 src[a * P:(a + 1) * P, bass.ds(g * GH, GH), :]).then_inc(xt_loaded[s], 16)
                src = bass.AP(tensor=kpad_dram.tensor, offset=0, ap=[[1, P], [KPAD, CH], [1, SUP]])
                sp.dma_start(toep[s][:, :, :], src[:, bass.ds(g * GH, GH), :]).then_inc(toep_loaded[s], 16)

            for s in range(SLOTS):
                load_group(s, s)

            def store_channels(i, first, last):
                for u in range(HPI):
                    h = i * HPI + u
                    sp.wait_ge(o_ready, h + 1)
                    for a in range(2):
                        for k in range(KA):
                            c0 = a * 1024 + k * SUP
                            sp.dma_start(out[:, bass.ds(h, 1), c0:c0 + SUP].rearrange("b a t -> (b a) t"),
                                         o_sb[u % 2][k * B:(k + 1) * B, a, :]).then_inc(o_stored[u % 2], 16)
                    if u % GH == GH - 1 and not last:
                        load_group((i + 1) * SLOTS + u // GH, u // GH)
            peeled(sp, NI2, store_channels)
            for s in range(2):
                sp.wait_ge(o_stored[s], 16 * 2 * KA * CH // 2)

        @block.gpsimd
        def _(pool):
            steps = [0]

            def link(ins):
                steps[0] += 1
                ins.then_inc(pool_step, 1)
                pool.wait_ge(pool_step, steps[0])

            for m in (ident, swap, zeros):
                link(pool.memset(m[:, :], 0.0))
            for m, off in ((ident, 0), (swap, MODES), (swap, -MODES)):
                link(pool.affine_select(out=m[:, :], in_=m[:, :], compare_op=ALU.not_equal, fill=1.0,
                                        base=off, pattern=[[-1, P]], channel_multiplier=1))
            link(pool.iota(part[:, :], [[0, 1]], base=0, channel_multiplier=1,
                           allow_small_or_imprecise_dtypes=True))
            link(pool.iota(time_row[:, :], [[1, L]], base=0, channel_multiplier=0,
                           allow_small_or_imprecise_dtypes=True))
            link(pool.iota(idx_b[:, :], [[1, 16]], base=1, channel_multiplier=0,
                           allow_small_or_imprecise_dtypes=True))
            link(pool.iota(idx_a[:, :], [[16, 16]], base=0, channel_multiplier=0,
                           allow_small_or_imprecise_dtypes=True))
            link(pool.memset(sgn[0:MODES, :], 1.0))
            link(pool.memset(sgn[MODES:P, :], -1.0))
            for k in range(KA):
                link(pool.memset(thr[k * B:(k + 1) * B, 0:1], float(-k * SUP)))
                link(pool.memset(thr[k * B:(k + 1) * B, 1:2], float(-k * SUP - 1024)))
            for m, top, low in ((z1, 1.0, 0.0), (z2, 0.0, 1.0)):
                link(pool.memset(m[0:MODES, :, 0:1], top))
                link(pool.memset(m[MODES:P, :, 0:1], low))
            link(pool.memset(s_sb[0][:, 0:B], 0.0))
            link(pool.memset(s_sb[1][:, 0:B], 0.0))
            pool.drain().then_inc(consts, 1)

            def split_batches(i, first, last):
                for u in range(BPI * NBLK):
                    n, s, q = i * BPI * NBLK + u, u // NBLK, u % NBLK
                    cols = slice(q * BLK, (q + 1) * BLK)
                    if q == 0:
                        pool.wait_ge(x_loaded[s], 16 * i + 16)
                        pool.wait_ge(w_ready, i * BPI + s + 1)
                    wait_apart(pool, mid_masked, n - 1)
                    pool.tensor_scalar(tmask[u % 2][:, :], time_row[:, cols], len_col[s][:, :], None,
                                       ALU.is_lt).then_inc(mask_ready, 1)
                    wait_apart(pool, hid_ready, 2 * n - 6)
                    pool.tensor_scalar(x_hi[:, q, :], x_in[s][:, cols], 1.0, None, ALU.mult).then_inc(x_high, 1)
                    pool.wait_ge(x_high, n + 1)
                    pool.tensor_tensor(x_lo[:, q, :], x_in[s][:, cols], x_hi[:, q, :],
                                       ALU.subtract).then_inc(x_split, 1)
            peeled(pool, NI1, split_batches)

            def powers(h, u):
                wait(pool, b_turned, h - 1)
                wait(pool, e_ready, h)
                pool.tensor_tensor(etmp[0][:, :, :], row_outer(l_re, h), row_bcast(z1, h),
                                   ALU.mult).then_inc(e_step, 1)
                pool.tensor_tensor(etmp[1][:, :, :], row_outer(l_im, h), row_bcast(z2, h),
                                   ALU.mult).then_inc(e_step, 1)
                pool.wait_ge(e_step, 2 * h + 2)
                pool.tensor_tensor(e_sb[u % 2][:, :, :], etmp[0][:, :, :], etmp[1][:, :, :],
                                   ALU.add).then_inc(e_ready, 1)

            def add_input(h, u):
                s, g = u // GH, u % GH
                pool.wait_ge(y_masked, h + 1)
                if not (isinstance(h, int) and h < 2):
                    pool.wait_ge(o_stored[u % 2], o_uses(h, u))
                pool.tensor_tensor(
                    o_sb[u % 2][:, :, :].rearrange("p a (c t) -> p a c t", t=T),
                    y_m[u % 2][:, :, :].rearrange("p a (c t) -> p a c t", t=T),
                    xt[s][:, :, g, :].rearrange("p a (c t) -> p a c t", t=T)[:, :, :, T - 1::-1],
                    ALU.add).then_inc(o_ready, 1)

            def o_uses(h, u):
                return (h - u % 2) * (16 * KA)

            pool.wait_ge(tables_ready, 1)
            powers(0, 0)
            powers(1, 1)

            def channels_pool(i, first, last):
                for u in range(HPI):
                    h = i * HPI + u
                    if not (last and u >= HPI - 2):
                        powers(h + 2, u)
                    if not (first and u == 0):
                        add_input(h - 1, (u - 1) % HPI)
            peeled(pool, NI2, channels_pool)
            add_input(CH - 1, HPI - 1)

        flat16 = "p (h r) -> p h r"
        scratch = [mid_out[0][:, :].rearrange(flat16, r=16), mid_out[1][:, :].rearrange(flat16, r=16),
                   g32[:, :, :, :].rearrange("p a b (c r) -> p (a b c) r", r=16)]

        @block.scalar
        def _(act):
            act.wait_ge(waves_in, 1)
            act.activation(hv[4][:, :], hv[2][:, :], ACT.Sin, scale=TWO_PI).then_inc(waves, 1)
            act.activation(hv[5][:, :], hv[2][:, :], ACT.Sin, scale=TWO_PI / 2).then_inc(waves, 1)
            act.activation(hv[6][:, :], par[:, 1, 0, :], ACT.Tanh, scale=-0.5).then_inc(waves, 1)
            for n, m in enumerate((q_sin, q_cos, l_im, l_re)):
                act.wait_ge(waves_in, 2 + n)
                act.activation(m[:, :, :], m[:, :, :], ACT.Sin, scale=TWO_PI).then_inc(waves, 1)
            for n, m in enumerate((rv[0], rv[1])):
                act.wait_ge(waves_in, 6 + n)
                act.activation(m[:, :], m[:, :], ACT.Sin, scale=TWO_PI).then_inc(waves, 1)
            for n, m in enumerate((scratch[2], scratch[0], rv[2][:, :])):
                act.wait_ge(waves_in, 8 + n)
                act.activation(m, m, ACT.Tanh, scale=-0.5).then_inc(waves, 1)
            act.wait_ge(consts, 1)
            act.wait_ge(waves_in, 11)
            for dst, src, rows, sign in ((z1, q_cos, slice(0, MODES), 1.0), (z1, q_sin, slice(MODES, P), 1.0),
                                         (z2, q_sin, slice(0, MODES), -1.0), (z2, q_cos, slice(MODES, P), 1.0)):
                act.activation(dst[rows, :, 1:16], src[rows, :, 0:15], ACT.Copy, scale=sign).then_inc(z_ready, 1)
            act.dma_start(kpad_dram[:, 0:T - 1], zeros[:, 0:T - 1]).then_inc(kpad_out, 16)
            act.wait_ge(kernel_ready, 1)
            act.dma_start(bass.AP(tensor=kpad_dram.tensor, offset=T - 1, ap=[[16, 16], [KPAD, CH], [1, 16]]),
                          scratch[1][0:16, :, :]).then_inc(kpad_out, 16)

            def gelus(i, first, last):
                for u in range(BPI * NBLK):
                    n = i * BPI * NBLK + u
                    wait(act, g_low, n - 1)
                    for h in range(2):
                        act.wait_ge(hid_ready, 2 * n + h + 1)
                        act.activation(g32[:, u % 2, h, :], hid_ps[u % 2][h][:, :], ACT.Gelu,
                                       bias=bias_col[u // NBLK][:, h:h + 1]
                                       ).then_inc(gelu_done, 1)
                    act.wait_ge(gelu_done, 2 * n + 2)
                    wait(act, mid_ready, n - 1)
                    act.activation(g_hi[u % 2][:, :, :], g32[:, u % 2, :, :], ACT.Copy).then_inc(g_high, 1)
            peeled(act, NI1, gelus)

            def evacuate(i, first, last):
                for u in range(HPI):
                    h = i * HPI + u
                    act.wait_ge(u_turned, h + 1)
                    wait(act, y_local, h - 1)
                    act.activation(u_sb[u % 2][:, :, :], up_ps[u % 2][:, :].rearrange("p (c k) -> p c k", c=2),
                                   ACT.Copy).then_inc(u_ready, 1)
                    act.wait_ge(b_turned, h + 1)
                    wait(act, v_done, h - 1)
                    act.activation(b_sb[u % 2][:, :, :],
                                   bt_ps[:, u % 2 * 256:u % 2 * 256 + 256].rearrange("p (c k) -> p c k", c=2),
                                   ACT.Copy).then_inc(b_ready, 1)
            peeled(act, NI2, evacuate)

        @block.vector
        def _(dve):
            done = {}

            def link(ins, s=None):
                s = s or dve_step
                done[s.name] = done.get(s.name, 0) + 1
                ins.then_inc(s, 1)
                dve.wait_ge(s, done[s.name])

            def ts(o, i, a, op0, b=None, op1=ALU.bypass, s=None):
                if b is None:
                    link(dve.tensor_scalar(o, i, a, None, op0), s)
                else:
                    link(dve.tensor_scalar(o, i, a, b, op0, op1), s)

            def tt(o, a, b, op, s=None):
                link(dve.tensor_tensor(o, a, b, op), s)

            def stt(o, a, c, op0, b, op1, s=None):
                link(dve.scalar_tensor_tensor(o, a, c, b, op0, op1), s)

            dve.wait_ge(params_in, 16 * (11 + KA))
            dve.wait_ge(consts, 1)
            link(dve.tensor_copy(onehot[:, :], sid8[:, :]))
            ts(onehot[:, :], onehot[:, :], part[0:SESS, :], ALU.is_equal, s=to_pe)
            link(dve.tensor_copy(ccf[:, :], cc_i[:, :]))
            ts(cmask[:, :], ccf[:, :], part[:, :], ALU.is_gt)
            link(dve.tensor_copy(lenf[:, :], len_i[:, :]))
            link(dve.tensor_copy(w2hi[:, :, :], w2_raw[:, :, :]))
            tt(w2lo[:, :, :], w2_raw[:, :, :], w2hi[:, :, :], ALU.subtract)
            link(dve.tensor_copy(rv[2][:, 0:1], olen_i[:, :]))
            ts(thr[:, :], thr[:, :], rv[2][:, 0:1], ALU.add)
            for a in range(2):
                ts(omask[:, a, :], time_row[:, 0:SUP], thr[:, a:a + 1], ALU.is_lt)

            n_, r_, q_, y_ = (e[:, :] for e in ex)
            ts(n_, expin[:, :], LOG2E, ALU.mult)
            ts(n_, n_, ROUND, ALU.add)
            ts(n_, n_, ROUND, ALU.subtract)
            ts(n_, n_, -126.0, ALU.max, 127.0, ALU.min)
            stt(r_, n_, -LN2_HI, ALU.mult, expin[:, :], ALU.add)
            stt(r_, n_, -LN2_LO, ALU.mult, r_, ALU.add)
            ts(q_, r_, 1.0 / 5040, ALU.mult)
            for k in (720, 120, 24, 6, 2, 1):
                stt(q_, q_, 1.0 / k, ALU.add, r_, ALU.mult)
            ts(ex_i[:, :], n_, 127.0, ALU.add, 2.0 ** 23, ALU.mult)
            stt(y_, q_, 1.0, ALU.add, ex_i[:, :].bitcast(F32), ALU.mult)
            ar, dt = ex[3][:, 0:MODES], ex[3][:, MODES:MODES + 1]

            h_ = [m[:, :] for m in hv]
            f, rho = par[:, 0, 0, :], par[:, 1, 0, :]
            ts(rho, ar, dt, ALU.mult)
            ts(f, aim[:, :], dt, ALU.mult, 1.0 / (2 * math.pi), ALU.mult)
            ts(h_[3], f, ROUND, ALU.add)
            ts(h_[3], h_[3], ROUND, ALU.subtract)
            tt(h_[2], f, h_[3], ALU.subtract, s=waves_in)
            tt(h_[7], ar, ar, ALU.mult)
            tt(h_[8], aim[:, :], aim[:, :], ALU.mult)
            tt(h_[7], h_[7], h_[8], ALU.add)
            link(dve.reciprocal(h_[7], h_[7]))
            dve.wait_ge(waves, 3)
            ts(h_[8], h_[6], -1.0, ALU.mult, 1.0, ALU.add)
            link(dve.reciprocal(h_[8], h_[8]))
            stt(h_[6], h_[6], 2.0, ALU.mult, h_[8], ALU.mult)
            stt(h_[5], h_[5], -2.0, ALU.mult, h_[5], ALU.mult)
            stt(h_[8], h_[5], 1.0, ALU.add, h_[6], ALU.mult)
            tt(h_[8], h_[8], h_[5], ALU.add)
            stt(h_[9], h_[6], 1.0, ALU.add, h_[4], ALU.mult)
            tt(h_[0], h_[8], ar, ALU.mult)
            tt(h_[1], h_[9], aim[:, :], ALU.mult)
            tt(h_[10], h_[1], h_[0], ALU.subtract)
            tt(h_[10], h_[10], h_[7], ALU.mult)
            tt(h_[0], h_[8], aim[:, :], ALU.mult)
            tt(h_[1], h_[9], ar, ALU.mult)
            stt(h_[11], h_[0], -1.0, ALU.mult, h_[1], ALU.subtract)
            tt(h_[11], h_[11], h_[7], ALU.mult)
            cr, ci = cc2[:, :, 0], cc2[:, :, 1]
            tt(h_[0], h_[10], cr, ALU.mult)
            tt(h_[1], h_[11], ci, ALU.mult)
            tt(h_[2], h_[0], h_[1], ALU.subtract)
            tt(h_[0], h_[11], cr, ALU.mult)
            tt(h_[1], h_[10], ci, ALU.mult)
            tt(h_[3], h_[0], h_[1], ALU.add)
            link(dve.tensor_copy(par[:, 0, 1, :], f))
            link(dve.tensor_copy(par[:, 1, 1, :], rho))
            ts(par[:, 2, 0, :], h_[2], 2.0, ALU.mult)
            ts(par[:, 2, 1, :], h_[3], -2.0, ALU.mult)
            ts(par[:, 3, 0, :], h_[3], -2.0, ALU.mult)
            ts(par[:, 3, 1, :], h_[2], -2.0, ALU.mult, s=to_pe)
            dve.wait_ge(pe_setup, 1)
            link(dve.tensor_copy(bias[:, :, :], bank[7][:, 0:2 * B].rearrange("p (c b) -> p b c", c=2)))
            dve.wait_ge(pe_setup, 2)
            link(dve.tensor_copy(par_t[:, :, :], bank[6][:, :].rearrange("p (c h) -> p c h", c=4)))
            f_t, rho_t, alpha, beta = (par_t[:, k, :] for k in range(4))

            def turns(t, whole, sine, cosine):
                ts(whole, t, ROUND, ALU.add)
                ts(whole, whole, ROUND, ALU.subtract)
                tt(sine, t, whole, ALU.subtract, s=waves_in)
                ts(t, t, 0.25, ALU.add)
                ts(whole, t, ROUND, ALU.add)
                ts(whole, whole, ROUND, ALU.subtract)
                tt(cosine, t, whole, ALU.subtract, s=waves_in)

            for idx, sine, cosine in ((idx_b, q_sin, q_cos), (idx_a, l_im, l_re)):
                tt(scratch[0], outer(f_t, 16), bcast(idx[:, :], CH), ALU.mult)
                turns(scratch[0], scratch[1], sine[:, :, :], cosine[:, :, :])
            ts(r_diag[:, :], f_t, float(SUP), ALU.mult)
            turns(r_diag[:, :], r_off[:, :], rv[0][:, :], rv[1][:, :])
            tt(scratch[2], outer(rho_t, 16), bcast(idx_b[:, :], CH), ALU.mult, s=waves_in)
            tt(scratch[0], outer(rho_t, 16), bcast(idx_a[:, :], CH), ALU.mult, s=waves_in)
            ts(rv[2][:, :], rho_t, float(SUP), ALU.mult, s=waves_in)

            def damp(t, d, n, sine, cosine, s=None):
                dve.wait_ge(waves, n)
                ts(d, t, -1.0, ALU.mult, 1.0, ALU.add)
                link(dve.reciprocal(d, d))
                stt(t, t, 1.0, ALU.add, d, ALU.mult)
                tt(sine, sine, t, ALU.mult)
                tt(cosine, cosine, t, ALU.mult, s=s)
            damp(scratch[2], scratch[1], 10, q_sin[:, :, :], q_cos[:, :, :], s=waves_in)
            damp(scratch[0], scratch[1], 11, l_im[:, :, :], l_re[:, :, :])
            damp(rv[2][:, :], r_off[:, :], 12, rv[0][:, :], rv[1][:, :])
            link(dve.tensor_copy(r_diag[:, :], rv[1][:, :]))
            ts(r_off[:, :], rv[0][:, :], sgn[:, :], ALU.mult)
            for dst, p, q, op in ((x1, alpha, beta, ALU.add), (x2, beta, alpha, ALU.subtract)):
                tt(scratch[0], l_re[:, :, :], outer(p, 16), ALU.mult)
                tt(scratch[1], l_im[:, :, :], outer(q, 16), ALU.mult)
                tt(dst[:, :, :], scratch[0], scratch[1], op, s=to_pe)
            dve.wait_ge(z_ready, 4)
            dve.wait_ge(pe_setup, 3)
            for k in range(4):
                link(dve.tensor_copy(scratch[1][0:16, k * 32:(k + 1) * 32, :],
                                     bank[k][0:16, :].rearrange("p (h r) -> p h r", r=16)))
            tt(scratch[1][0:1, :, 0], scratch[1][0:1, :, 0], d_row[:, :], ALU.add, s=kernel_ready)
            dve.drain().then_inc(tables_ready, 1)

            def weights(b, s):
                dve.wait_ge(w_loaded[s], w_count(b, s))
                wait(dve, hid_ready, 2 * NBLK * (b - 1))
                wait(dve, w_ready, b)
                keep = cmask[:, bass.ds(b, 1)]
                dve.tensor_scalar(w_m[:, :], w_raw[s][:, :], keep, None, ALU.mult).then_inc(w_step, 1)
                dve.tensor_copy(len_col[s][:, :], lenf[:, bass.ds(b, 1)])
                dve.tensor_copy(bias_col[s][:, :], bias[:, bass.ds(b, 1), :].rearrange("p a h -> p (a h)"))
                dve.wait_ge(w_step, 2 * b + 1)
                dve.tensor_copy(w_hi[s][:, :], w_m[:, :]).then_inc(w_step, 1)
                dve.wait_ge(w_step, 2 * b + 2)
                dve.tensor_tensor(w_lo[s][:, :], w_m[:, :], w_hi[s][:, :], ALU.subtract).then_inc(w_ready, 1)

            def w_count(b, s):
                return (b - s) * (16 // BPI) + 16

            def finish_block(n, u):
                s, q = u // NBLK, u % NBLK
                cols = slice(q * BLK, (q + 1) * BLK)
                dve.wait_ge(mid_ready, n + 1)
                dve.wait_ge(mask_ready, n + 1)
                wait(dve, mid_added, n - 1)
                dve.scalar_tensor_tensor(mid_m[u % 2][:, :], mid_ps[u % 2][:, :], b2_col[:, :], tmask[u % 2][:, :],
                                         ALU.add, ALU.mult).then_inc(mid_masked, 1)
                dve.wait_ge(mid_masked, n + 1)
                dve.tensor_tensor(
                    mid_out[s][:, cols].rearrange("p (c t) -> p c t", t=T)[:, :, T - 1::-1],
                    mid_m[u % 2][:, :].rearrange("p (c t) -> p c t", t=T),
                    x_in[s][:, cols].rearrange("p (c t) -> p c t", t=T), ALU.add).then_inc(mid_added, 1)

            def blocks(i, first, last):
                for u in range(BPI * NBLK):
                    n, b = i * BPI * NBLK + u, i * BPI + u // NBLK
                    if u % NBLK == NBLK - 1 and not (last and u == BPI * NBLK - 1):
                        weights(b + 1, (u // NBLK + 1) % BPI)
                    dve.wait_ge(g_high, n + 1)
                    wait(dve, mid_ready, n - 1)
                    dve.tensor_tensor(g_lo[u % 2][:, :, :], g32[:, u % 2, :, :], g_hi[u % 2][:, :, :],
                                      ALU.subtract).then_inc(g_low, 1)
                    if first and u in (1, NBLK + 1):
                        dve.wait_ge(kpad_out, 32)
                    if not first and (u - 1) % NBLK == 0:
                        dve.wait_ge(mid_stored[(u - 1) // NBLK], 16 * i)
                    if not (first and u == 0):
                        finish_block(n - 1, (u - 1) % (BPI * NBLK))
            weights(0, 0)
            peeled(dve, NI1, blocks)
            finish_block(B * NBLK - 1, BPI * NBLK - 1)

            def transition(h, u, half):
                if half == 0:
                    wait(dve, state_added, 6 * (h - 1))
                    dve.tensor_scalar(r_sb[u % 2][:, :], ident[:, :], r_diag[:, bass.ds(h, 1)], None,
                                      ALU.mult).then_inc(r_step, 1)
                else:
                    dve.wait_ge(r_step, h + 1)
                    dve.scalar_tensor_tensor(r_sb[u % 2][:, :], swap[:, :], r_off[:, bass.ds(h, 1)],
                                             r_sb[u % 2][:, :], ALU.mult, ALU.add).then_inc(r_ready, 1)

            def outputs_of_state(h, u, part_):
                if part_ < 2:
                    if part_ == 0:
                        wait(dve, c_ready, h)
                    left, right = ((x1, q_cos), (x2, q_sin))[part_]
                    dve.tensor_tensor(ctmp[part_][:, :, :], row_outer(left, h), row_bcast(right, h),
                                      ALU.mult).then_inc(c_step, 1)
                else:
                    dve.wait_ge(c_step, 2 * h + 2)
                    wait(dve, y_done, h - 1)
                    dve.tensor_tensor(c_sb[u % 2][:, :, :], ctmp[0][:, :, :], ctmp[1][:, :, :],
                                      ALU.add).then_inc(c_ready, 1)

            def keep_state(k, h, u):
                if k == 1:
                    dve.wait_ge(v_done, h + 1)
                    wait(dve, y_done, h - 1)
                else:
                    dve.wait_ge(state_added, 6 * h + k - 1)
                dve.tensor_copy(s_sb[u % 2][:, k * B:(k + 1) * B],
                                v_ps[u % 2][:, (k - 1) * B:k * B]).then_inc(state_ready, 1)

            def mask_output(h, u):
                dve.wait_ge(y_done, h + 1)
                wait(dve, o_ready, h - 1)
                dve.tensor_tensor(y_m[u % 2][:, :, :], y_ps[u % 2][:, :].rearrange("p (a t) -> p a t", a=2),
                                  omask[:, :, :], ALU.mult).then_inc(y_masked, 1)

            transition(0, 0, 0)
            transition(0, 0, 1)
            keep_state(1, 0, 0)

            def channels_dve(i, first, last):
                for u in range(HPI):
                    h = i * HPI + u
                    end = last and u == HPI - 1
                    for k in range(2, NSUP):
                        keep_state(k, h, u)
                        if k < 4 and not end:
                            transition(h + 1, u + 1, k - 2)
                        if k >= 4 and k < 7:
                            outputs_of_state(h, u, k - 4)
                    if not (first and u == 0):
                        mask_output(h - 1, u + 1)
                    if not end:
                        keep_state(1, h + 1, u + 1)
            peeled(dve, NI2, channels_dve)
            mask_output(CH - 1, HPI - 1)

        @block.tensor
        def _(pe):
            pe.wait_ge(to_pe, 1)
            for h in range(2):
                ins = pe.matmul(bank[7][:, h * B:(h + 1) * B], bs_raw[:, h * P:(h + 1) * P], onehot[:, :],
                                start=True, stop=True)
            ins.then_inc(pe_setup, 1)
            pe.wait_ge(to_pe, 2)
            for k in range(4):
                ins = pe.transpose(bank[6][:, k * CH:(k + 1) * CH], par[:, k, :, :].rearrange("p a m -> p (a m)"),
                                   ident[:, :])
            ins.then_inc(pe_setup, 1)
            pe.wait_ge(to_pe, 3)
            pe.wait_ge(z_ready, 4)
            for h in range(CH):
                ins = pe.matmul(bank[h // 32][0:16, h % 32 * 16:h % 32 * 16 + 16], x1[:, h, :], z1[:, h, :],
                                start=True, stop=True)
            ins.then_inc(pe_setup, 1)
            pe.wait_ge(tables_ready, 1)

            def hidden(i, n, u):
                s, q = u // NBLK, u % NBLK
                pe.wait_ge(x_split, n + 1)
                if q == 0:
                    pe.wait_ge(w_ready, i * BPI + s + 1)
                for h in range(2):
                    wait(pe, gelu_done, 2 * n - 3 + h)
                    cols = slice(h * P, (h + 1) * P)
                    o = hid_ps[u % 2][h][:, :]
                    pe.matmul(o, w_hi[s][:, cols], x_hi[:, q, :], start=True, stop=False)
                    pe.matmul(o, w_hi[s][:, cols], x_lo[:, q, :], start=False, stop=False)
                    pe.matmul(o, w_lo[s][:, cols], x_hi[:, q, :], start=False, stop=True).then_inc(hid_ready, 1)

            def project(n, u):
                pe.wait_ge(g_low, n + 1)
                wait(pe, mid_masked, n - 1)
                o = mid_ps[u % 2][:, :]
                for h in range(2):
                    pe.matmul(o, w2hi[:, h, :], g_hi[u % 2][:, h, :], start=h == 0, stop=False)
                    pe.matmul(o, w2lo[:, h, :], g_hi[u % 2][:, h, :], start=False, stop=False)
                    ins = pe.matmul(o, w2hi[:, h, :], g_lo[u % 2][:, h, :], start=False, stop=h == 1)
                ins.then_inc(mid_ready, 1)

            def blocks_pe(i, first, last):
                for u in range(BPI * NBLK):
                    n = i * BPI * NBLK + u
                    hidden(i, n, u)
                    if not (first and u == 0):
                        project(n - 1, (u - 1) % (BPI * NBLK))
            peeled(pe, NI1, blocks_pe)
            project(B * NBLK - 1, BPI * NBLK - 1)

            def turn(i, h, u):
                s, g = u // GH, u % GH
                if g == 0:
                    pe.wait_ge(xt_loaded[s], 32 * i + 32)
                wait(pe, u_ready, h - 1)
                for c in range(2):
                    for a in range(2):
                        o = (c * 2 + a) * P
                        ins = pe.transpose(up_ps[u % 2][:, o:o + P], xt[s][:, a, g, c * T:(c + 1) * T], ident[:, :])
                ins.then_inc(u_turned, 1)
                pe.wait_ge(e_ready, h + 1)
                wait(pe, b_ready, h - 1)
                powers = e_sb[u % 2][:, :, :].rearrange("p a b -> p (a b)")
                for c in range(2):
                    o = u % 2 * 256 + c * P
                    ins = pe.transpose(bt_ps[:, o:o + P], powers[:, c * T:(c + 1) * T], ident[:, :])
                ins.then_inc(b_turned, 1)

            def state_inputs(h, u):
                pe.wait_ge(u_ready, h + 1)
                pe.wait_ge(b_ready, h + 1)
                wait(pe, state_ready, 7 * (h - 1))
                o = v_ps[u % 2][:, 0:7 * B]
                pe.matmul(o, b_sb[u % 2][:, 1, :], u_sb[u % 2][:, 0, 0:7 * B], start=True, stop=False)
                pe.matmul(o, b_sb[u % 2][:, 0, :], u_sb[u % 2][:, 1, 0:7 * B], start=False,
                          stop=True).then_inc(v_done, 1)

            def carry(k, h, u):
                if k == 1:
                    pe.wait_ge(r_ready, h + 1)
                pe.wait_ge(state_ready, 7 * h + k)
                pe.matmul(v_ps[u % 2][:, k * B:(k + 1) * B], r_sb[u % 2][:, :], s_sb[u % 2][:, k * B:(k + 1) * B],
                          start=False, stop=True, skip_group_check=True).then_inc(state_added, 1)

            def local(i, h, u, a):
                s, g = u // GH, u % GH
                if a == 0:
                    wait(pe, y_masked, h - 1)
                    if g == 0:
                        pe.wait_ge(toep_loaded[s], 16 * i + 16)
                y, us = y_ps[u % 2], u_sb[u % 2]
                o = a * SUP
                pe.matmul(y[:, o:o + SUP], us[:, 0, a * P:(a + 1) * P], toep[s][:, g, :],
                          start=a == 0, stop=False, skip_group_check=True)
                ins = pe.matmul(y[:, o + T:o + SUP], us[:, 1, a * P:(a + 1) * P], toep[s][:, g, 0:T],
                                start=False, stop=False, skip_group_check=True)
                if a == 1:
                    ins.then_inc(y_local, 1)

            def from_state(h, u, a):
                if a == 0:
                    pe.wait_ge(c_ready, h + 1)
                    pe.wait_ge(state_ready, 7 * h + 7)
                ins = pe.matmul(y_ps[u % 2][:, a * SUP:(a + 1) * SUP], s_sb[u % 2][:, a * P:(a + 1) * P],
                                c_sb[u % 2][:, :, :].rearrange("p a b -> p (a b)"),
                                start=False, stop=True, skip_group_check=True)
                if a == 1:
                    ins.then_inc(y_done, 1)

            pe.wait_ge(gelu_done, 2 * B * NBLK)
            pe.wait_ge(mid_masked, B * NBLK)
            turn(0, 0, 0)
            state_inputs(0, 0)

            def channels_pe(i, first, last):
                for u in range(HPI):
                    h = i * HPI + u
                    end = last and u == HPI - 1
                    nxt = (u + 1) % HPI
                    carry(1, h, u)
                    if not end:
                        turn(i + (1 if nxt == 0 else 0), h + 1, nxt)
                    carry(2, h, u)
                    if not (first and u == 0):
                        from_state(h - 1, u + 1, 0)
                    carry(3, h, u)
                    if not (first and u == 0):
                        from_state(h - 1, u + 1, 1)
                    carry(4, h, u)
                    local(i, h, u, 0)
                    carry(5, h, u)
                    local(i, h, u, 1)
                    carry(6, h, u)
                    if not end:
                        state_inputs(h + 1, u + 1)
            peeled(pe, NI2, channels_pe)
            for a in range(2):
                from_state(CH - 1, HPI - 1, a)


_INS = ["x", "itok_B_0_7", "itok_B_2182_4065", "itok_B_78_3631", "_lenS", "L0_cond_W_sess", "L0_cond_b_sess",
        "L0_cond_W2", "L0_cond_b2", "L1_cond_log_dt", "L1_cond_C", "L1_cond_log_A_real", "L1_cond_A_imag",
        "L1_cond_D"]


def kernel(**inputs):
    import numpy as _np
    import concourse.bacc as _bacc
    from concourse import mybir as _mybir
    from concourse.bass_utils import run_bass_kernel_spmd as _run

    nc = _bacc.Bacc("TRN2", target_bir_lowering=False, num_devices=1)
    arrays, args = {}, []
    for name in _INS:
        a = _np.ascontiguousarray(inputs[name])
        arrays[f"in_{name}_dram"] = a
        args.append(nc.dram_tensor(f"in_{name}_dram", a.shape, _mybir.dt.from_np(a.dtype), kind="ExternalInput").ap())
    out = nc.dram_tensor("out_dram", (B, CH, L), _mybir.dt.float32, kind="ExternalOutput").ap()
    session_and_state_space_layer(nc, *args, out)
    r = _run(nc, [arrays], core_ids=[0])
    return r.results[0]["out_dram"]
```

```python
import math
from contextlib import ExitStack

import concourse.bass as bass
from concourse import mybir

F32 = mybir.dt.float32
BF16 = mybir.dt.bfloat16
I32 = mybir.dt.int32
ACT = mybir.ActivationFunctionType
ALU = mybir.AluOpType

P = 128
B, CH, L = 32, 128, 2048
HID, SESS, MODES = 256, 8, 64
T = 128
SUP = 2 * T
NSUP = L // SUP
BLK = 512
NBLK = L // BLK
NPAR = 6
F, RHO, ALPHA, BETA, GAIN_D, GAIN_O = range(NPAR)
KPAD = 3 * T

LOG2E = math.log2(math.e)
LN2_HI = 0.693359375
LN2_LO = math.log(2.0) - LN2_HI
ROUND = 1.5 * 2.0 ** 23
TWO_PI = 6.283185


def session_and_state_space_layer(nc, x, sid, seq_len, out_len, chan_count, w_sess, b_sess, w2, b2,
                                  log_dt, c_in, log_a, a_imag, d_in, out):
    ctx = ExitStack()
    with ctx:
        def sb(name, shape, dt=F32):
            return ctx.enter_context(nc.sbuf_tensor(name, shape, dt))

        def sem(name):
            return ctx.enter_context(nc.semaphore(name))

        def pair(name, shape, dt=F32, n=2):
            return [sb(f"{name}{i}", shape, dt) for i in range(n)]

        mid_dram = nc.dram_tensor("mid_scratch", [NSUP, B, CH, SUP], F32, kind="Internal").ap()
        kpad_dram = nc.dram_tensor("kernel_scratch", [CH, 2, KPAD], BF16, kind="Internal").ap()

        expin = sb("expin", [P, MODES + 1])
        aim = sb("aim", [P, MODES])
        cc2 = sb("cc2", [P, MODES, 2])
        d_rows = sb("d_rows", [P, CH // 4])
        w2_raw = sb("w2_raw", [P, 2, CH])
        b2_col = sb("b2_col", [P, 1])
        bs_raw = sb("bs_raw", [SESS, HID])
        sid8 = sb("sid8", [SESS, B], I32)
        cc_i = sb("cc_i", [P, B], I32)
        len_i = sb("len_i", [P, B], I32)
        olen_i = sb("olen_i", [P, 1], I32)
        sid_row = sb("sid_row", [1, B], I32)

        ident = sb("ident", [P, P])
        swap = sb("swap", [P, P])
        part = sb("part", [P, 1])
        time_row = sb("time_row", [P, L])
        sgn = sb("sgn", [P, 1])
        zeros = sb("zeros", [P, 2, T], BF16)

        onehot = sb("onehot", [SESS, B])
        ccf = sb("ccf", [P, B])
        cmask = sb("cmask", [P, B])
        lenf = sb("lenf", [P, B])
        bias = sb("bias", [P, B, 2])
        w2hi = sb("w2hi", [P, 2, CH], BF16)
        w2lo = sb("w2lo", [P, 2, CH], BF16)

        ex = [sb(f"ex{i}", [P, MODES + 1]) for i in range(4)]
        ex_i = sb("ex_i", [P, MODES + 1], I32)
        hv = [sb(f"hv{i}", [P, MODES]) for i in range(12)]
        par = sb("par", [P, NPAR, 2, MODES])
        par_t = sb("par_t", [P, NPAR, CH])
        l_re = sb("l_re", [P, 16, CH])
        l_im = sb("l_im", [P, 16, CH])
        z1 = sb("z1", [P, 16, CH])
        z2 = sb("z2", [P, 16, CH])
        x1 = sb("x1", [P, 16, CH])
        seed = sb("seed", [P, 3, CH])
        seed_re = sb("seed_re", [P, 3, CH])
        seed_im = sb("seed_im", [P, 3, CH])
        seed_t = [sb(f"seed_t{i}", [P, 3, CH]) for i in range(2)]
        r_off = sb("r_off", [P, CH])
        taps = sb("taps", [P, CH // 4, 16])
        taps_half = sb("taps_half", [P, 2, CH // 4, 16], BF16)
        thr = sb("thr", [P, 2])
        omask = sb("omask", [P, 2, SUP])

        x_in = pair("x_in", [P, L])
        mid_out = pair("mid_out", [P, L])
        x_hi = sb("x_hi", [P, 4, BLK], BF16)
        x_lo = sb("x_lo", [P, 4, BLK], BF16)
        w_raw = pair("w_raw", [P, HID])
        w_m = sb("w_m", [P, HID])
        w_hi = pair("w_hi", [P, HID], BF16)
        w_lo = pair("w_lo", [P, HID], BF16)
        len_col = pair("len_col", [P, 1])
        bias_col = pair("bias_col", [P, 2])
        g32 = sb("g32", [P, 2, 2, BLK])
        g_hi = pair("g_hi", [P, 2, BLK], BF16)
        g_lo = pair("g_lo", [P, 2, BLK], BF16)
        tmask = pair("tmask", [P, BLK])
        mid_m = pair("mid_m", [P, BLK])

        SLOTS, GH = 4, 2
        xt = [x_in[s // 2][:, s % 2 * 1024:s % 2 * 1024 + 1024].rearrange(
            "p (a g t) -> p a g t", a=2, g=GH) for s in range(SLOTS)]
        toep = [mid_out[0][:, s * 512:s * 512 + 512].bitcast(BF16).rearrange(
            "p (g c t) -> p g c t", g=GH, c=2) for s in range(SLOTS)]
        u_hi = pair("u_hi", [P, 2, SUP], BF16, n=4)
        u_lo = pair("u_lo", [P, 2, SUP], BF16, n=4)
        b_hi = sb("b_hi", [P, 2, SUP], BF16)
        b_lo = sb("b_lo", [P, 2, SUP], BF16)
        s32 = pair("s32", [P, 2, SUP])
        s_hi = pair("s_hi", [P, 2, SUP], BF16)
        s_lo = pair("s_lo", [P, 2, SUP], BF16)
        e32 = pair("e32", [P, 2, 16, 16], n=4)
        e_hi = pair("e_hi", [P, 2, SUP], BF16)
        e_lo = pair("e_lo", [P, 2, SUP], BF16)
        etmp = pair("etmp", [P, 2, 16, 16])
        r_sb = pair("r_sb", [P, 2, P])
        gain = sb("gain", [P, 2, P])
        y_m = pair("y_m", [P, 2, SUP])
        o_sb = pair("o_sb", [P, 2, SUP])

        bank = [ctx.enter_context(nc.psum_tensor(f"bank{i}", [P, 512], F32)) for i in range(8)]
        hid_ps = [[bank[2 * i + h] for h in range(2)] for i in range(2)]
        mid_ps = [bank[4], bank[5]]
        up_ps = bank[0]
        bt_ps = bank[1]
        v_ps = [bank[2][:, :].rearrange("p (c k) -> p c k", c=2), bank[3][:, :].rearrange("p (c k) -> p c k", c=2)]
        y_ps = [bank[4], bank[5], bank[6], bank[7]]

        params_in = sem("params_in")
        sid_in = sem("sid_in")
        consts = sem("consts")
        pool_step = sem("pool_step")
        dve_step = sem("dve_step")
        waves_in = sem("waves_in")
        waves = sem("waves")
        to_pe = sem("to_pe")
        pe_setup = sem("pe_setup")
        tables_ready = sem("tables_ready")
        kernel_ready = sem("kernel_ready")
        kpad_out = sem("kpad_out")
        x_loaded = [[sem(f"x_loaded{i}_{j}") for j in range(2)] for i in range(2)]
        w_loaded = [sem(f"w_loaded{i}") for i in range(2)]
        w_step = sem("w_step")
        w_ready = sem("w_ready")
        x_high = sem("x_high")
        x_low = sem("x_low")
        mask_ready = sem("mask_ready")
        hid_ready = sem("hid_ready")
        gelu_done = sem("gelu_done")
        g_high = sem("g_high")
        g_low = sem("g_low")
        mid_ready = sem("mid_ready")
        mid_masked = sem("mid_masked")
        mid_added = sem("mid_added")
        mid_stored = [[sem(f"mid_stored{i}_{j}") for j in range(2)] for i in range(2)]
        xt_loaded = [sem(f"xt_loaded{i}") for i in range(SLOTS)]
        toep_loaded = [sem(f"toep_loaded{i}") for i in range(SLOTS)]
        u_turned = sem("u_turned")
        u_high = sem("u_high")
        u_low = sem("u_low")
        y_local = sem("y_local")
        y_done = sem("y_done")
        y_masked = sem("y_masked")
        o_ready = sem("o_ready")
        o_stored = [sem(f"o_stored{i}") for i in range(2)]
        b_made = sem("b_made")
        b_high = sem("b_high")
        b_low = sem("b_low")
        e_step = sem("e_step")
        e_ready = sem("e_ready")
        e_high = sem("e_high")
        e_low = sem("e_low")
        r_step = sem("r_step")
        r_ready = sem("r_ready")
        gain_step = sem("gain_step")
        gain_ready = sem("gain_ready")
        v_done = sem("v_done")
        state_added = sem("state_added")
        state_first = sem("state_first")
        state_ready = sem("state_ready")
        s_high = sem("s_high")
        s_low = sem("s_low")

        block = ctx.enter_context(nc.Block())

        def wait(eng, s, value):
            if not isinstance(value, int) or value > 0:
                eng.wait_ge(s, value)

        def peeled(eng, count, body):
            body(0, True, False)
            with eng.Fori(1, count - 1) as i:
                body(i, False, False)
            body(count - 1, False, True)

        def pair_row(table, j, n, outer):
            v = table[:, :, bass.ds(j * GH, GH)].rearrange("p r g -> p g r")
            return v.unsqueeze(3).to_broadcast([P, GH, 16, n]) if outer else v.unsqueeze(2).to_broadcast([P, GH, n, 16])

        BPI = 2
        NI1 = B // BPI
        HPI = SLOTS * GH
        NI2 = CH // HPI
        PPI = SLOTS
        KA = 1024 // SUP

        @block.sync
        def _(sp):
            sp.dma_start(sid_row[:, :], sid.rearrange("(a n) -> a n", a=1)).then_inc(sid_in, 16)
            for dst, src in (
                (expin[:, 0:MODES], log_a), (expin[:, MODES:MODES + 1], log_dt.rearrange("(p a) -> p a", a=1)),
                (aim[:, :], a_imag), (cc2[:, :, :], c_in), 
                (w2_raw[:, :, :], w2.rearrange("(a p) s -> p a s", p=P)),
                (b2_col[:, :], b2.rearrange("(p a) -> p a", a=1)), (bs_raw[:, :], b_sess),
                (sid8[:, :], sid.partition_broadcast(SESS)), (cc_i[:, :], chan_count.partition_broadcast(P)),
                (len_i[:, :], seq_len.partition_broadcast(P)),
            ):
                sp.dma_start(dst, src).then_inc(params_in, 16)
            for g in range(4):
                sp.dma_start(d_rows[32 * g:32 * g + 1, :],
                             d_in[g * 32:(g + 1) * 32].rearrange("(a n) -> a n", a=1)).then_inc(params_in, 16)
            for k in range(KA):
                sp.dma_start(olen_i[k * B:(k + 1) * B, :],
                             out_len.rearrange("(p a) -> p a", a=1)).then_inc(params_in, 16)

            sp.wait_ge(sid_in, 16)

            HALF = L // 2

            def load_half(b, s, half):
                sp.dma_start(x_in[s][:, half * HALF:(half + 1) * HALF],
                             x[bass.ds(b, 1), :, half * HALF:(half + 1) * HALF].rearrange("a c t -> (a c) t")
                             ).then_inc(x_loaded[s][half], 16)
                if half == 0:
                    session = sp.value_load(sid_row[0:1, bass.ds(b, 1)], min_val=0, max_val=SESS - 1)
                    sp.dma_start(w_raw[s][:, :], w_sess[bass.ds(session, 1), :, :].rearrange("a c h -> (a c) h")
                                 ).then_inc(w_loaded[s], 16)

            for s in range(BPI):
                for half in range(2):
                    load_half(s, s, half)

            def store_halves(i, first, last):
                for s in range(BPI):
                    b = i * BPI + s
                    for half in range(2):
                        sp.wait_ge(mid_added, NBLK * b + 2 * half + 2)
                        k0 = half * NSUP // 2
                        sp.dma_start(
                            mid_dram[k0:k0 + NSUP // 2, bass.ds(b, 1), :, :].rearrange("k a c t -> c (k a) t"),
                            mid_out[s][:, half * HALF:(half + 1) * HALF].rearrange("c (k t) -> c k t", t=SUP)
                        ).then_inc(mid_stored[s][half], 16)
                        if not last:
                            load_half(b + BPI, s, half)
            peeled(sp, NI1, store_halves)
            for s in range(BPI):
                for half in range(2):
                    sp.wait_ge(mid_stored[s][half], 16 * NI1)
            sp.wait_ge(kpad_out, 16 * 9)

            def load_group(g, s):
                for a in range(2):
                    src = bass.AP(tensor=mid_dram.tensor, offset=0,
                                  ap=[[CH * SUP, NSUP * B], [SUP, CH], [1, SUP]])
                    sp.dma_start(xt[s][:, a, :, :],
                                 src[a * P:(a + 1) * P, bass.ds(g * GH, GH), :]).then_inc(xt_loaded[s], 16)
                src = bass.AP(tensor=kpad_dram.tensor, offset=0, ap=[[1, P], [KPAD, 2 * CH], [1, SUP]])
                sp.dma_start(toep[s][:, :, :, :].rearrange("p g c t -> p (g c) t"),
                             src[:, bass.ds(g * 2 * GH, 2 * GH), :]).then_inc(toep_loaded[s], 16)

            for s in range(SLOTS):
                load_group(s, s)

            def store_channels(i, first, last):
                for u in range(HPI):
                    h = i * HPI + u
                    sp.wait_ge(o_ready, h + 1)
                    for a in range(2):
                        for k in range(KA):
                            c0 = a * 1024 + k * SUP
                            sp.dma_start(out[:, bass.ds(h, 1), c0:c0 + SUP].rearrange("b a t -> (b a) t"),
                                         o_sb[u % 2][k * B:(k + 1) * B, a, :]).then_inc(o_stored[u % 2], 16)
                    if u % GH == GH - 1 and not last:
                        load_group((i + 1) * SLOTS + u // GH, u // GH)
            peeled(sp, NI2, store_channels)
            for s in range(2):
                sp.wait_ge(o_stored[s], 16 * 2 * KA * CH // 2)

        @block.gpsimd
        def _(pool):
            steps = [0]

            def link(ins):
                steps[0] += 1
                ins.then_inc(pool_step, 1)
                pool.wait_ge(pool_step, steps[0])

            for m in (ident[:, :], swap[:, :], zeros[:, :, :], taps[:, :, :]):
                link(pool.memset(m, 0.0))
            for m, off in ((ident, 0), (swap, MODES), (swap, -MODES)):
                link(pool.affine_select(out=m[:, :], in_=m[:, :], compare_op=ALU.not_equal, fill=1.0,
                                        base=off, pattern=[[-1, P]], channel_multiplier=1))
            link(pool.iota(part[:, :], [[0, 1]], base=0, channel_multiplier=1,
                           allow_small_or_imprecise_dtypes=True))
            link(pool.iota(time_row[:, :], [[1, L]], base=0, channel_multiplier=0,
                           allow_small_or_imprecise_dtypes=True))
            link(pool.memset(sgn[0:MODES, :], -1.0))
            link(pool.memset(sgn[MODES:P, :], 1.0))
            for k in range(KA):
                link(pool.memset(thr[k * B:(k + 1) * B, 0:1], float(-k * SUP)))
                link(pool.memset(thr[k * B:(k + 1) * B, 1:2], float(-k * SUP - 1024)))
            for m in s32:
                link(pool.memset(m[:, :, 0:B], 0.0))
            pool.drain().then_inc(consts, 1)

            def low_half(i, u):
                n, s, q = i * BPI * NBLK + u, u // NBLK % BPI, u % NBLK
                pool.wait_ge(x_high, n + 1)
                pool.tensor_tensor(x_lo[:, q, :], x_in[s][:, q * BLK:(q + 1) * BLK], x_hi[:, q, :],
                                   ALU.subtract).then_inc(x_low, 1)

            def add_x(i, u):
                n, s, q = i * BPI * NBLK + u, u // NBLK % BPI, u % NBLK
                cols = slice(q * BLK, (q + 1) * BLK)
                pool.wait_ge(mid_masked, n + 1)
                if q % 2 == 0:
                    wait(pool, mid_stored[s][q // 2], 16 * i)
                pool.tensor_tensor(
                    mid_out[s][:, cols].rearrange("p (c t) -> p c t", t=T)[:, :, T - 1::-1],
                    mid_m[u % 2][:, :].rearrange("p (c t) -> p c t", t=T),
                    x_in[s][:, cols].rearrange("p (c t) -> p c t", t=T), ALU.add).then_inc(mid_added, 1)

            low_half(0, 0)
            low_half(0, 1)

            def blocks_pool(i, first, last):
                for u in range(BPI * NBLK):
                    if not (last and u >= BPI * NBLK - 2):
                        low_half(i, u + 2)
                    if u > 0:
                        add_x(i, u - 1)
                    elif not first:
                        add_x(i - 1, BPI * NBLK - 1)
            peeled(pool, NI1, blocks_pool)
            add_x(NI1 - 1, BPI * NBLK - 1)

            def powers(j, q):
                wait(pool, e_low, j - 3)
                wait(pool, e_ready, j)
                pool.tensor_tensor(etmp[0][:, :, :, :], pair_row(l_re, j, 16, True), pair_row(z1, j, 16, False),
                                   ALU.mult).then_inc(e_step, 1)
                pool.tensor_tensor(etmp[1][:, :, :, :], pair_row(l_im, j, 16, True), pair_row(z2, j, 16, False),
                                   ALU.mult).then_inc(e_step, 1)
                pool.wait_ge(e_step, 2 * j + 2)
                pool.tensor_tensor(e32[q][:, :, :, :], etmp[0][:, :, :, :], etmp[1][:, :, :, :],
                                   ALU.add).then_inc(e_ready, 1)

            def state_low(j, q):
                pool.wait_ge(s_high, j + 1)
                pool.tensor_tensor(s_lo[q % 2][:, :, :], s32[q % 2][:, :, :], s_hi[q % 2][:, :, :],
                                   ALU.subtract).then_inc(s_low, 1)

            def add_input(h, u):
                s, g = u // GH, u % GH
                pool.wait_ge(y_masked, h + 1)
                wait(pool, o_stored[u % 2], (h - u % 2) * (16 * KA))
                pool.tensor_tensor(
                    o_sb[u % 2][:, :, :].rearrange("p a (c t) -> p a c t", t=T),
                    y_m[u % 2][:, :, :].rearrange("p a (c t) -> p a c t", t=T),
                    xt[s][:, :, g, :].rearrange("p a (c t) -> p a c t", t=T)[:, :, :, T - 1::-1],
                    ALU.add).then_inc(o_ready, 1)

            pool.wait_ge(tables_ready, 1)
            powers(0, 0)
            powers(1, 1)

            def pairs_pool(i, first, last):
                for q in range(PPI):
                    j = i * PPI + q
                    start = first and q == 0
                    if not start:
                        state_low(j - 1, q + 1)
                    if not (last and q >= PPI - 2):
                        powers(j + 2, (q + 2) % PPI)
                    if not start:
                        for g in range(GH):
                            add_input(GH * (j - 1) + g, (GH * (q - 1) + g) % HPI)
            peeled(pool, NI2, pairs_pool)
            state_low(CH // GH - 1, PPI - 1)
            for g in range(GH):
                add_input(CH - GH + g, HPI - GH + g)

        @block.scalar
        def _(act):
            act.wait_ge(waves_in, 1)
            act.activation(hv[4][:, :], hv[2][:, :], ACT.Sin, scale=TWO_PI).then_inc(waves, 1)
            act.activation(hv[5][:, :], hv[2][:, :], ACT.Sin, scale=TWO_PI / 2).then_inc(waves, 1)
            act.activation(hv[6][:, :], par[:, RHO, 0, :], ACT.Tanh, scale=-0.5).then_inc(waves, 1)
            act.wait_ge(waves_in, 2)
            act.activation(seed[:, :, :], seed[:, :, :], ACT.Tanh, scale=-0.5).then_inc(waves, 1)
            act.wait_ge(waves_in, 4)
            act.activation(seed_im[:, :, :], seed_im[:, :, :], ACT.Sin, scale=TWO_PI).then_inc(waves, 1)
            act.activation(seed_re[:, :, :], seed_re[:, :, :], ACT.Sin, scale=TWO_PI).then_inc(waves, 1)
            def store_kernel():
                act.wait_ge(consts, 1)
                act.dma_start(kpad_dram[:, :, 0:T - 1], zeros[:, :, 0:T - 1]).then_inc(kpad_out, 16)
                act.wait_ge(kernel_ready, 1)
                for g in range(4):
                    for half in range(2):
                        act.dma_start(bass.AP(tensor=kpad_dram.tensor, offset=(g * 32 * 2 + half) * KPAD + T - 1,
                                              ap=[[16, 16], [2 * KPAD, 32], [1, 16]]),
                                      taps_half[32 * g:32 * g + 16, half, :, :]).then_inc(kpad_out, 16)

            def gelus(i, first, last):
                for u in range(BPI * NBLK):
                    n = i * BPI * NBLK + u
                    wait(act, g_low, n - 1)
                    for h in range(2):
                        act.wait_ge(hid_ready, 2 * n + h + 1)
                        act.activation(g32[:, u % 2, h, :], hid_ps[u % 2][h][:, :], ACT.Gelu,
                                       bias=bias_col[u // NBLK][:, h:h + 1]
                                       ).then_inc(gelu_done, 1)
                    act.wait_ge(gelu_done, 2 * n + 2)
                    wait(act, mid_ready, n - 1)
                    act.activation(g_hi[u % 2][:, :, :], g32[:, u % 2, :, :], ACT.Copy).then_inc(g_high, 1)
                if first:
                    store_kernel()
            peeled(act, NI1, gelus)

            def high(dst, src, s):
                act.activation(dst, src, ACT.Copy).then_inc(s, 1)

            def state_high(j, q):
                act.wait_ge(state_ready, 6 * j + 6)
                wait(act, y_done, GH * (j - 1))
                high(s_hi[q % 2][:, :, :], s32[q % 2][:, :, :], s_high)

            def input_high(h, u):
                act.wait_ge(u_turned, h + 1)
                wait(act, y_local, h - 3)
                high(u_hi[u % 4][:, :, :], up_ps[:, :].rearrange("p (c k) -> p c k", c=2), u_high)

            def matrix_high(j):
                act.wait_ge(b_made, j + 1)
                wait(act, v_done, j)
                high(b_hi[:, :, :], bt_ps[:, :].rearrange("p (g c) -> p g c", g=GH), b_high)

            def halves(i, first, last):
                for q in range(PPI):
                    j = i * PPI + q
                    if not (first and q == 0):
                        state_high(j - 1, q + 1)
                    if not (last and q == PPI - 1):
                        for g in range(GH):
                            input_high(GH * (j + 1) + g, GH * (q + 1) + g)
                        matrix_high(j + 1)
                    act.wait_ge(e_ready, j + 1)
                    wait(act, y_done, GH * (j - 1))
                    high(e_hi[q % 2][:, :, :], e32[q][:, :, :, :].rearrange("p g a b -> p g (a b)"), e_high)
            for g in range(GH):
                input_high(g, g)
            matrix_high(0)
            peeled(act, NI2, halves)
            state_high(CH // GH - 1, PPI - 1)

        @block.vector
        def _(dve):
            done = {}

            def link(ins, s=None):
                s = s or dve_step
                done[s.name] = done.get(s.name, 0) + 1
                ins.then_inc(s, 1)
                dve.wait_ge(s, done[s.name])

            def ts(o, i, a, op0, b=None, op1=ALU.bypass, s=None):
                if b is None:
                    link(dve.tensor_scalar(o, i, a, None, op0), s)
                else:
                    link(dve.tensor_scalar(o, i, a, b, op0, op1), s)

            def tt(o, a, b, op, s=None):
                link(dve.tensor_tensor(o, a, b, op), s)

            def stt(o, a, c, op0, b, op1, s=None):
                link(dve.scalar_tensor_tensor(o, a, c, b, op0, op1), s)

            dve.wait_ge(params_in, 16 * (10 + 4 + KA))
            dve.wait_ge(consts, 1)
            link(dve.tensor_copy(onehot[:, :], sid8[:, :]))
            ts(onehot[:, :], onehot[:, :], part[0:SESS, :], ALU.is_equal, s=to_pe)
            link(dve.tensor_copy(ccf[:, :], cc_i[:, :]))
            ts(cmask[:, :], ccf[:, :], part[:, :], ALU.is_gt)
            link(dve.tensor_copy(lenf[:, :], len_i[:, :]))
            link(dve.tensor_copy(w2hi[:, :, :], w2_raw[:, :, :]))
            tt(w2lo[:, :, :], w2_raw[:, :, :], w2hi[:, :, :], ALU.subtract)
            link(dve.tensor_copy(r_off[:, 0:1], olen_i[:, :]))
            ts(thr[:, :], thr[:, :], r_off[:, 0:1], ALU.add)
            for a in range(2):
                ts(omask[:, a, :], time_row[:, 0:SUP], thr[:, a:a + 1], ALU.is_lt)

            n_, r_, q_, y_ = (e[:, :] for e in ex)
            ts(n_, expin[:, :], LOG2E, ALU.mult, ROUND, ALU.add)
            ts(n_, n_, ROUND, ALU.subtract)
            ts(n_, n_, -126.0, ALU.max, 127.0, ALU.min)
            stt(r_, n_, -LN2_HI, ALU.mult, expin[:, :], ALU.add)
            stt(r_, n_, -LN2_LO, ALU.mult, r_, ALU.add)
            ts(q_, r_, 1.0 / 5040, ALU.mult)
            for k in (720, 120, 24, 6, 2, 1):
                stt(q_, q_, 1.0 / k, ALU.add, r_, ALU.mult)
            ts(ex_i[:, :], n_, 127.0, ALU.add, 2.0 ** 23, ALU.mult)
            stt(y_, q_, 1.0, ALU.add, ex_i[:, :].bitcast(F32), ALU.mult)
            ar, dt = ex[3][:, 0:MODES], ex[3][:, MODES:MODES + 1]

            h_ = [m[:, :] for m in hv]
            f, rho = par[:, F, 0, :], par[:, RHO, 0, :]
            ts(rho, ar, dt, ALU.mult)
            ts(f, aim[:, :], dt, ALU.mult, 1.0 / (2 * math.pi), ALU.mult)
            ts(h_[3], f, ROUND, ALU.add)
            ts(h_[3], h_[3], ROUND, ALU.subtract)
            tt(h_[2], f, h_[3], ALU.subtract, s=waves_in)
            tt(h_[7], ar, ar, ALU.mult)
            tt(h_[8], aim[:, :], aim[:, :], ALU.mult)
            tt(h_[7], h_[7], h_[8], ALU.add)
            link(dve.reciprocal(h_[7], h_[7]))
            dve.wait_ge(waves, 3)
            ts(h_[8], h_[6], -1.0, ALU.mult, 1.0, ALU.add)
            link(dve.reciprocal(h_[8], h_[8]))
            stt(h_[6], h_[6], 2.0, ALU.mult, h_[8], ALU.mult)
            stt(h_[5], h_[5], -2.0, ALU.mult, h_[5], ALU.mult)
            stt(h_[8], h_[5], 1.0, ALU.add, h_[6], ALU.mult)
            tt(h_[8], h_[8], h_[5], ALU.add)
            stt(h_[9], h_[6], 1.0, ALU.add, h_[4], ALU.mult)
            tt(h_[0], h_[8], ar, ALU.mult)
            tt(h_[1], h_[9], aim[:, :], ALU.mult)
            tt(h_[10], h_[1], h_[0], ALU.subtract)
            tt(h_[10], h_[10], h_[7], ALU.mult)
            tt(h_[0], h_[8], aim[:, :], ALU.mult)
            tt(h_[1], h_[9], ar, ALU.mult)
            stt(h_[11], h_[0], -1.0, ALU.mult, h_[1], ALU.subtract)
            tt(h_[11], h_[11], h_[7], ALU.mult)
            cr, ci = cc2[:, :, 0], cc2[:, :, 1]
            tt(h_[0], h_[10], cr, ALU.mult)
            tt(h_[1], h_[11], ci, ALU.mult)
            tt(h_[2], h_[0], h_[1], ALU.subtract)
            tt(h_[0], h_[11], cr, ALU.mult)
            tt(h_[1], h_[10], ci, ALU.mult)
            tt(h_[3], h_[0], h_[1], ALU.add)
            ts(h_[8], h_[8], 1.0, ALU.add)
            tt(h_[0], h_[2], h_[8], ALU.mult)
            tt(h_[1], h_[3], h_[9], ALU.mult)
            tt(h_[6], h_[0], h_[1], ALU.subtract)
            tt(h_[0], h_[2], h_[9], ALU.mult)
            tt(h_[1], h_[3], h_[8], ALU.mult)
            tt(h_[7], h_[0], h_[1], ALU.add)
            link(dve.tensor_copy(par[:, F, 1, :], f))
            link(dve.tensor_copy(par[:, RHO, 1, :], rho))
            ts(par[:, ALPHA, 0, :], h_[2], 2.0, ALU.mult)
            ts(par[:, ALPHA, 1, :], h_[3], -2.0, ALU.mult)
            ts(par[:, BETA, 0, :], h_[3], -2.0, ALU.mult)
            ts(par[:, BETA, 1, :], h_[2], -2.0, ALU.mult)
            ts(par[:, GAIN_D, 0, :], h_[6], 2.0, ALU.mult)
            ts(par[:, GAIN_D, 1, :], h_[6], -2.0, ALU.mult)
            ts(par[:, GAIN_O, 0, :], h_[7], -2.0, ALU.mult)
            ts(par[:, GAIN_O, 1, :], h_[7], -2.0, ALU.mult, s=to_pe)
            dve.wait_ge(pe_setup, 1)
            link(dve.tensor_copy(bias[:, :, :], bank[7][:, 0:2 * B].rearrange("p (c b) -> p b c", c=2)))
            dve.wait_ge(pe_setup, 2)
            for k in range(2):
                link(dve.tensor_copy(par_t[:, 3 * k:3 * k + 3, :],
                                     bank[5 + k][:, 0:3 * CH].rearrange("p (c h) -> p c h", c=3)))
            alpha, beta = par_t[:, ALPHA, :], par_t[:, BETA, :]

            POWERS = (1.0, 16.0, float(SUP))
            turns, whole = (m[:, :, :] for m in seed_t)
            for k, r in enumerate(POWERS):
                ts(seed[:, k, :], par_t[:, RHO, :], r, ALU.mult, s=waves_in if k == 2 else None)
            for k, r in enumerate(POWERS):
                ts(turns[:, k, :], par_t[:, F, :], r, ALU.mult)
            for dst in (seed_im, seed_re):
                ts(whole, turns, ROUND, ALU.add)
                ts(whole, whole, ROUND, ALU.subtract)
                tt(dst[:, :, :], turns, whole, ALU.subtract, s=waves_in)
                if dst is seed_im:
                    ts(turns, turns, 0.25, ALU.add)
            dve.wait_ge(waves, 4)
            ts(whole, seed[:, :, :], -1.0, ALU.mult, 1.0, ALU.add)
            link(dve.reciprocal(whole, whole))
            stt(seed[:, :, :], seed[:, :, :], 1.0, ALU.add, whole, ALU.mult)
            dve.wait_ge(waves, 6)
            tt(seed_im[:, :, :], seed_im[:, :, :], seed[:, :, :], ALU.mult)
            tt(seed_re[:, :, :], seed_re[:, :, :], seed[:, :, :], ALU.mult)
            ts(r_off[:, :], seed_im[:, 2, :], sgn[:, :], ALU.mult)

            tmp = [m[:, :].rearrange("p (r h) -> p r h", h=CH) for m in mid_out]

            def powers_of(k, re, im):
                link(dve.memset(re[:, 0, :], 1.0))
                link(dve.memset(im[:, 0, :], 0.0))
                link(dve.tensor_copy(re[:, 1, :], seed_re[:, k, :]))
                link(dve.tensor_copy(im[:, 1, :], seed_im[:, k, :]))
                for n, m in ((1, 1), (2, 2), (4, 4), (8, 7)):
                    top_re = re[:, n, :].unsqueeze(1).to_broadcast([P, m, CH])
                    top_im = im[:, n, :].unsqueeze(1).to_broadcast([P, m, CH])
                    low, new, t = slice(1, m + 1), slice(n + 1, n + m + 1), slice(0, m)
                    dve.tensor_tensor(tmp[0][:, t, :], re[:, low, :], top_re, ALU.mult)
                    tt(tmp[1][:, t, :], im[:, low, :], top_im, ALU.mult)
                    tt(re[:, new, :], tmp[0][:, t, :], tmp[1][:, t, :], ALU.subtract)
                    dve.tensor_tensor(tmp[0][:, t, :], re[:, low, :], top_im, ALU.mult)
                    tt(tmp[1][:, t, :], im[:, low, :], top_re, ALU.mult)
                    tt(im[:, new, :], tmp[0][:, t, :], tmp[1][:, t, :], ALU.add)
            powers_of(1, l_re[:, :, :], l_im[:, :, :])
            row = lambda p: p.unsqueeze(1).to_broadcast([P, 16, CH])
            dve.tensor_tensor(tmp[0], l_re[:, :, :], row(alpha), ALU.mult)
            tt(tmp[1], l_im[:, :, :], row(beta), ALU.mult)
            tt(x1[:, :, :], tmp[0], tmp[1], ALU.add)
            powers_of(0, z1[:, :, :], z2[:, :, :])
            top, low = slice(0, MODES), slice(MODES, P)
            link(dve.tensor_copy(tmp[0][low], z1[low, :, :]))
            link(dve.tensor_copy(z1[low, :, :], z2[low, :, :]))
            link(dve.tensor_copy(z2[low, :, :], tmp[0][low]))
            ts(z2[top, :, :], z2[top, :, :], -1.0, ALU.mult, s=to_pe)

            def kernel_taps():
                dve.wait_ge(pe_setup, 3)
                for g in range(4):
                    rows = slice(32 * g, 32 * g + 16)
                    link(dve.tensor_copy(taps[rows, :, :], bank[7][rows, :].rearrange("p (h r) -> p h r", r=16)))
                    one = slice(32 * g, 32 * g + 1)
                    tt(taps[one, :, 0], taps[one, :, 0], d_rows[one, :], ALU.add)
                link(dve.tensor_copy(taps_half[:, 0, :, :], taps[:, :, :]))
                tt(taps_half[:, 1, :, :], taps[:, :, :], taps_half[:, 0, :, :], ALU.subtract, s=kernel_ready)
                dve.drain().then_inc(tables_ready, 1)

            def weights(b, s):
                dve.wait_ge(w_loaded[s], w_count(b, s))
                wait(dve, hid_ready, 2 * NBLK * (b - 1))
                wait(dve, w_ready, b)
                keep = cmask[:, bass.ds(b, 1)]
                dve.tensor_scalar(w_m[:, :], w_raw[s][:, :], keep, None, ALU.mult).then_inc(w_step, 1)
                dve.tensor_copy(len_col[s][:, :], lenf[:, bass.ds(b, 1)])
                dve.tensor_copy(bias_col[s][:, :], bias[:, bass.ds(b, 1), :].rearrange("p a h -> p (a h)"))
                dve.wait_ge(w_step, 2 * b + 1)
                dve.tensor_copy(w_hi[s][:, :], w_m[:, :]).then_inc(w_step, 1)
                dve.wait_ge(w_step, 2 * b + 2)
                dve.tensor_tensor(w_lo[s][:, :], w_m[:, :], w_hi[s][:, :], ALU.subtract).then_inc(w_ready, 1)

            def w_count(b, s):
                return (b - s) * (16 // BPI) + 16

            def high_half(i, u):
                n, s, q = i * BPI * NBLK + u, u // NBLK % BPI, u % NBLK
                if q % 2 == 0:
                    dve.wait_ge(x_loaded[s][q // 2], 16 * i + 16 + 16 * (u // (BPI * NBLK)))
                wait(dve, hid_ready, 2 * n - 6)
                dve.tensor_copy(x_hi[:, q, :], x_in[s][:, q * BLK:(q + 1) * BLK]).then_inc(x_high, 1)

            def time_mask(n, u):
                cols = slice(u % NBLK * BLK, (u % NBLK + 1) * BLK)
                wait(dve, mid_masked, n - 1)
                dve.tensor_scalar(tmask[u % 2][:, :], time_row[:, cols], len_col[u // NBLK][:, :], None,
                                  ALU.is_lt).then_inc(mask_ready, 1)

            def mask_block(n, u):
                dve.wait_ge(mid_ready, n + 1)
                dve.wait_ge(mask_ready, n + 1)
                wait(dve, mid_added, n - 1)
                dve.scalar_tensor_tensor(mid_m[u % 2][:, :], mid_ps[u % 2][:, :], b2_col[:, :], tmask[u % 2][:, :],
                                         ALU.add, ALU.mult).then_inc(mid_masked, 1)

            def blocks(i, first, last):
                for u in range(BPI * NBLK):
                    n, b = i * BPI * NBLK + u, i * BPI + u // NBLK
                    if u % NBLK == NBLK - 1 and not (last and u == BPI * NBLK - 1):
                        weights(b + 1, (u // NBLK + 1) % BPI)
                    if not (last and u >= BPI * NBLK - 2):
                        high_half(i, u + 2)
                    dve.wait_ge(g_high, n + 1)
                    wait(dve, mid_ready, n - 1)
                    dve.tensor_tensor(g_lo[u % 2][:, :, :], g32[:, u % 2, :, :], g_hi[u % 2][:, :, :],
                                      ALU.subtract).then_inc(g_low, 1)
                    if not (first and u == 0):
                        mask_block(n - 1, (u - 1) % (BPI * NBLK))
                    time_mask(n, u)
                    if first and u == NBLK - 1:
                        kernel_taps()
            weights(0, 0)
            high_half(0, 0)
            high_half(0, 1)
            peeled(dve, NI1, blocks)
            mask_block(B * NBLK - 1, BPI * NBLK - 1)

            def blend(dst, diag, off, j, q, step, s):
                for g in range(GH):
                    dve.tensor_scalar(dst[:, g, :], ident[:, :], diag[:, bass.ds(GH * j + g, 1)], None,
                                      ALU.mult).then_inc(step, 1)
                for g in range(GH):
                    dve.wait_ge(step, GH * j + g + 1)
                    dve.scalar_tensor_tensor(dst[:, g, :], swap[:, :], off[:, bass.ds(GH * j + g, 1)], dst[:, g, :],
                                             ALU.mult, ALU.add).then_inc(s, 1)

            def transition(j, q):
                wait(dve, state_added, 6 * (j - 1))
                blend(r_sb[q % 2], seed_re[:, 2, :], r_off[:, :], j, q, r_step, r_ready)

            def gains(j, q):
                wait(dve, b_made, j)
                blend(gain, par_t[:, GAIN_D, :], par_t[:, GAIN_O, :], j, q, gain_step, gain_ready)

            def keep_state(k, j, q):
                if k == 1:
                    dve.wait_ge(v_done, j + 1)
                    wait(dve, s_low, j - 1)
                else:
                    dve.wait_ge(state_added, 6 * j + k - 1)
                dve.tensor_copy(s32[q % 2][:, :, k * B:(k + 1) * B],
                                v_ps[q % 2][:, :, (k - 1) * B:k * B]).then_inc(state_first if k == 1 else state_ready, 1)

            def input_low(h, u):
                dve.wait_ge(u_high, h + 1)
                dve.tensor_tensor(u_lo[u % 4][:, :, :], up_ps[:, :].rearrange("p (c k) -> p c k", c=2),
                                  u_hi[u % 4][:, :, :], ALU.subtract).then_inc(u_low, 1)

            def matrix_low(j):
                dve.wait_ge(b_high, j + 1)
                dve.tensor_tensor(b_lo[:, :, :], bt_ps[:, :].rearrange("p (g c) -> p g c", g=GH), b_hi[:, :, :],
                                  ALU.subtract).then_inc(b_low, 1)

            def powers_low(j, q):
                dve.wait_ge(e_high, j + 1)
                dve.tensor_tensor(e_lo[q % 2][:, :, :], e32[q][:, :, :, :].rearrange("p g a b -> p g (a b)"),
                                  e_hi[q % 2][:, :, :], ALU.subtract).then_inc(e_low, 1)

            def mask_output(h, u):
                dve.wait_ge(y_done, h + 1)
                wait(dve, o_ready, h - 1)
                dve.tensor_tensor(y_m[u % 2][:, :, :], y_ps[u % 4][:, :].rearrange("p (a t) -> p a t", a=2),
                                  omask[:, :, :], ALU.mult).then_inc(y_masked, 1)

            gains(0, 0)
            transition(0, 0)
            input_low(0, 0)
            input_low(1, 1)
            matrix_low(0)
            keep_state(1, 0, 0)

            def pairs_dve(i, first, last):
                for q in range(PPI):
                    j = i * PPI + q
                    start, end = first and q == 0, last and q == PPI - 1
                    h, u = GH * j, GH * q
                    keep_state(2, j, q)
                    if not end:
                        gains(j + 1, q + 1)
                    keep_state(3, j, q)
                    if not end:
                        input_low(h + 2, u + 2)
                    keep_state(4, j, q)
                    if not end:
                        input_low(h + 3, u + 3)
                    keep_state(5, j, q)
                    if not end:
                        matrix_low(j + 1)
                    if not start:
                        mask_output(h - 2, u + 2)
                    keep_state(6, j, q)
                    if not start:
                        mask_output(h - 1, u + 3)
                    if not end:
                        keep_state(1, j + 1, q + 1)
                    keep_state(7, j, q)
                    powers_low(j, q)
                    if not end:
                        transition(j + 1, q + 1)
            peeled(dve, NI2, pairs_dve)
            for g in range(GH):
                mask_output(CH - GH + g, HPI - GH + g)

        @block.tensor
        def _(pe):
            pe.wait_ge(to_pe, 1)
            for h in range(2):
                ins = pe.matmul(bank[7][:, h * B:(h + 1) * B], bs_raw[:, h * P:(h + 1) * P], onehot[:, :],
                                start=True, stop=True)
            ins.then_inc(pe_setup, 1)
            pe.wait_ge(to_pe, 2)
            for k in range(NPAR):
                ins = pe.transpose(bank[5 + k // 3][:, k % 3 * CH:(k % 3 + 1) * CH],
                                   par[:, k, :, :].rearrange("p a m -> p (a m)"), ident[:, :])
            ins.then_inc(pe_setup, 1)
            pe.wait_ge(to_pe, 3)
            for h in range(CH):
                g, c = h // 32, h % 32 * 16
                ins = pe.matmul(bank[7][32 * g:32 * g + 16, c:c + 16], x1[:, :, h], z1[:, :, h],
                                start=True, stop=True)
            ins.then_inc(pe_setup, 1)

            def hidden(i, n, u):
                s, q = u // NBLK, u % NBLK
                pe.wait_ge(x_low, n + 1)
                if q == 0:
                    pe.wait_ge(w_ready, i * BPI + s + 1)
                for h in range(2):
                    wait(pe, gelu_done, 2 * n - 3 + h)
                    cols = slice(h * P, (h + 1) * P)
                    o = hid_ps[u % 2][h][:, :]
                    pe.matmul(o, w_hi[s][:, cols], x_hi[:, q, :], start=True, stop=False)
                    pe.matmul(o, w_hi[s][:, cols], x_lo[:, q, :], start=False, stop=False)
                    pe.matmul(o, w_lo[s][:, cols], x_hi[:, q, :], start=False, stop=True).then_inc(hid_ready, 1)

            def project(n, u):
                pe.wait_ge(g_low, n + 1)
                wait(pe, mid_masked, n - 1)
                o = mid_ps[u % 2][:, :]
                for h in range(2):
                    pe.matmul(o, w2hi[:, h, :], g_hi[u % 2][:, h, :], start=h == 0, stop=False)
                    pe.matmul(o, w2lo[:, h, :], g_hi[u % 2][:, h, :], start=False, stop=False)
                    ins = pe.matmul(o, w2hi[:, h, :], g_lo[u % 2][:, h, :], start=False, stop=h == 1)
                ins.then_inc(mid_ready, 1)

            def blocks_pe(i, first, last):
                for u in range(BPI * NBLK):
                    n = i * BPI * NBLK + u
                    hidden(i, n, u)
                    if not (first and u == 0):
                        project(n - 1, (u - 1) % (BPI * NBLK))
            peeled(pe, NI1, blocks_pe)
            project(B * NBLK - 1, BPI * NBLK - 1)

            def three(out_, left_hi, left_lo, right_hi, right_lo, start, stop, skip=False):
                pe.matmul(out_, left_hi, right_hi, start=start, stop=False, skip_group_check=skip)
                pe.matmul(out_, left_hi, right_lo, start=False, stop=False, skip_group_check=skip)
                return pe.matmul(out_, left_lo, right_hi, start=False, stop=stop, skip_group_check=skip)

            def turn(i, h, u):
                s, g = u // GH, u % GH
                if g == 0:
                    pe.wait_ge(xt_loaded[s], 32 * i + 32)
                wait(pe, u_low, h)
                for c in range(2):
                    for a in range(2):
                        o = (c * 2 + a) * P
                        ins = pe.transpose(up_ps[:, o:o + P], xt[s][:, a, g, c * T:(c + 1) * T], ident[:, :])
                ins.then_inc(u_turned, 1)

            def input_matrices(j, q):
                pe.wait_ge(e_ready, j + 1)
                pe.wait_ge(gain_ready, GH * j + GH)
                wait(pe, b_low, j)
                for g in range(GH):
                    e = e32[q][:, g, :, :].rearrange("p a b -> p (a b)")
                    for c in range(2):
                        o = g * SUP + c * P
                        ins = pe.matmul(bt_ps[:, o:o + P], e[:, c * T:(c + 1) * T], gain[:, g, :],
                                        start=True, stop=True)
                ins.then_inc(b_made, 1)

            def state_inputs(j, q):
                pe.wait_ge(u_low, GH * j + GH)
                pe.wait_ge(b_low, j + 1)
                wait(pe, state_ready, 6 * (j - 1))
                for g in range(GH):
                    k = q % 2 * 2 + g
                    o = v_ps[q % 2][:, g, 0:7 * B]
                    three(o, b_hi[:, g, P:2 * P], b_lo[:, g, P:2 * P], u_hi[k][:, 0, 0:7 * B], u_lo[k][:, 0, 0:7 * B],
                          start=g == 0, stop=False, skip=g == 1)
                    ins = three(o, b_hi[:, g, 0:P], b_lo[:, g, 0:P], u_hi[k][:, 1, 0:7 * B],
                                u_lo[k][:, 1, 0:7 * B], start=False, stop=True, skip=g == 1)
                ins.then_inc(v_done, 1)

            def carry(k, j, q):
                if k == 1:
                    pe.wait_ge(r_ready, GH * j + GH)
                if k == 1:
                    pe.wait_ge(state_first, j + 1)
                else:
                    pe.wait_ge(state_ready, 6 * j + k - 1)
                for g in range(GH):
                    ins = pe.matmul(v_ps[q % 2][:, g, k * B:(k + 1) * B], r_sb[q % 2][:, g, :],
                                    s32[q % 2][:, g, k * B:(k + 1) * B], start=False, stop=True, skip_group_check=True)
                ins.then_inc(state_added, 1)

            def local(i, j, q, g, a):
                k = q % 2 * 2 + g
                if a == 0:
                    wait(pe, y_masked, GH * j + g - 3)
                    if g == 0:
                        pe.wait_ge(toep_loaded[q], 16 * i + 16)
                y, t = y_ps[k], toep[q]
                o, cols = a * SUP, slice(a * P, (a + 1) * P)
                three(y[:, o:o + SUP], u_hi[k][:, 0, cols], u_lo[k][:, 0, cols], t[:, g, 0, :], t[:, g, 1, :],
                      start=a == 0, stop=False, skip=True)
                ins = three(y[:, o + T:o + SUP], u_hi[k][:, 1, cols], u_lo[k][:, 1, cols], t[:, g, 0, 0:T],
                            t[:, g, 1, 0:T], start=False, stop=False, skip=True)
                if a == 1:
                    ins.then_inc(y_local, 1)

            def from_state(j, q, g):
                if g == 0:
                    pe.wait_ge(e_low, j + 1)
                    pe.wait_ge(s_low, j + 1)
                for a in range(2):
                    cols = slice(a * P, (a + 1) * P)
                    ins = three(y_ps[q % 2 * 2 + g][:, a * SUP:(a + 1) * SUP], s_hi[q % 2][:, g, cols],
                                s_lo[q % 2][:, g, cols], e_hi[q % 2][:, g, :], e_lo[q % 2][:, g, :],
                                start=False, stop=True, skip=True)
                ins.then_inc(y_done, 1)

            pe.wait_ge(tables_ready, 1)
            pe.wait_ge(gelu_done, 2 * B * NBLK)
            pe.wait_ge(mid_masked, B * NBLK)
            for g in range(GH):
                turn(0, g, g)
            input_matrices(0, 0)
            state_inputs(0, 0)

            def pairs_pe(i, first, last):
                for q in range(PPI):
                    j = i * PPI + q
                    start, end = first and q == 0, last and q == PPI - 1
                    nq = (q + 1) % PPI
                    ni = i + 1 if nq == 0 else i
                    carry(1, j, q)
                    if not end:
                        turn(ni, GH * (j + 1), GH * nq)
                    local(i, j, q, 0, 0)
                    carry(2, j, q)
                    if not end:
                        turn(ni, GH * (j + 1) + 1, GH * nq + 1)
                    local(i, j, q, 0, 1)
                    for g in range(GH):
                        carry(3 + g, j, q)
                        if not start:
                            from_state(j - 1, q + 1, g)
                        if g == 0 and not end:
                            input_matrices(j + 1, nq)
                    carry(5, j, q)
                    if not end:
                        state_inputs(j + 1, q + 1)
                    carry(6, j, q)
                    for a in range(2):
                        local(i, j, q, 1, a)
            peeled(pe, NI2, pairs_pe)
            for g in range(GH):
                from_state(CH // GH - 1, PPI - 1, g)


_INS = ["x", "itok_B_0_7", "itok_B_2182_4065", "itok_B_78_3631", "_lenS", "L0_cond_W_sess", "L0_cond_b_sess",
        "L0_cond_W2", "L0_cond_b2", "L1_cond_log_dt", "L1_cond_C", "L1_cond_log_A_real", "L1_cond_A_imag",
        "L1_cond_D"]


def kernel(**inputs):
    import numpy as _np
    import concourse.bacc as _bacc
    from concourse import mybir as _mybir
    from concourse.bass_utils import run_bass_kernel_spmd as _run

    nc = _bacc.Bacc("TRN2", target_bir_lowering=False, num_devices=1)
    arrays, args = {}, []
    for name in _INS:
        a = _np.ascontiguousarray(inputs[name])
        arrays[f"in_{name}_dram"] = a
        args.append(nc.dram_tensor(f"in_{name}_dram", a.shape, _mybir.dt.from_np(a.dtype), kind="ExternalInput").ap())
    out = nc.dram_tensor("out_dram", (B, CH, L), _mybir.dt.float32, kind="ExternalOutput").ap()
    session_and_state_space_layer(nc, *args, out)
    r = _run(nc, [arrays], core_ids=[0])
    return r.results[0]["out_dram"]
```

```python
import math
from contextlib import ExitStack

import concourse.bass as bass
from concourse import mybir

F32 = mybir.dt.float32
BF16 = mybir.dt.bfloat16
I32 = mybir.dt.int32
ACT = mybir.ActivationFunctionType
ALU = mybir.AluOpType

P = 128
B, CH, L = 32, 128, 2048
HID, SESS, MODES = 256, 8, 64
T = 128
SUP = 2 * T
NSUP = L // SUP
BLK = 512
NBLK = L // BLK
NPAR = 6
F, RHO, ALPHA, BETA, GAIN_D, GAIN_O = range(NPAR)
KPAD = 3 * T

LOG2E = math.log2(math.e)
LN2_HI = 0.693359375
LN2_LO = math.log(2.0) - LN2_HI
POWERS = (1.0, 16.0, float(SUP))
NPOW = len(POWERS)
ROUND = 1.5 * 2.0 ** 23
TWO_PI = 6.283185


def session_and_state_space_layer(nc, x, sid, seq_len, out_len, chan_count, w_sess, b_sess, w2, b2,
                                  log_dt, c_in, log_a, a_imag, d_in, out):
    ctx = ExitStack()
    with ctx:
        def sb(name, shape, dt=F32):
            return ctx.enter_context(nc.sbuf_tensor(name, shape, dt))

        def sem(name):
            return ctx.enter_context(nc.semaphore(name))

        def pair(name, shape, dt=F32, n=2):
            return [sb(f"{name}{i}", shape, dt) for i in range(n)]

        mid_dram = nc.dram_tensor("mid_scratch", [NSUP // 2, B, CH, 2 * SUP], F32, kind="Internal").ap()
        kpad_dram = nc.dram_tensor("kernel_scratch", [CH, 2, KPAD], BF16, kind="Internal").ap()

        expin = sb("expin", [P, MODES + 1])
        aim = sb("aim", [P, MODES])
        cc2 = sb("cc2", [P, MODES, 2])
        d_rows = sb("d_rows", [P, CH // 4])
        w2_raw = sb("w2_raw", [P, 2, CH])
        b2_col = sb("b2_col", [P, 1])
        bs_raw = sb("bs_raw", [SESS, HID])
        sid8 = sb("sid8", [SESS, B], I32)
        cc_i = sb("cc_i", [P, B], I32)
        len_i = sb("len_i", [P, B], I32)
        olen_i = sb("olen_i", [P, 1], I32)
        sid_row = sb("sid_row", [1, B], I32)

        ident = sb("ident", [P, P])
        swap = sb("swap", [P, P])
        part = sb("part", [P, 1])
        time_row = sb("time_row", [P, L])
        sgn = sb("sgn", [P, 1])
        zeros = sb("zeros", [P, 2, T], BF16)

        onehot = sb("onehot", [SESS, B])
        ccf = sb("ccf", [P, B])
        batch_t = sb("batch_t", [P, B, 4])
        w2hi = sb("w2hi", [P, 2, CH], BF16)
        w2lo = sb("w2lo", [P, 2, CH], BF16)

        ex = [sb(f"ex{i}", [P, MODES + 1]) for i in range(4)]
        ex_i = sb("ex_i", [P, MODES + 1], I32)
        hv = [sb(f"hv{i}", [P, MODES]) for i in range(12)]
        par = sb("par", [P, NPAR, 2, MODES])
        par_t = sb("par_t", [P, NPAR, CH])
        l_re = sb("l_re", [P, 16, CH])
        l_im = sb("l_im", [P, 16, CH])
        z1 = sb("z1", [P, 16, CH])
        z2 = sb("z2", [P, 16, CH])
        x1 = sb("x1", [P, 16, CH])
        seed = sb("seed", [P, NPOW, CH])
        seed_re = sb("seed_re", [P, NPOW, CH])
        seed_im = sb("seed_im", [P, NPOW, CH])
        seed_t = [sb(f"seed_t{i}", [P, NPOW, CH]) for i in range(2)]
        blend_t = sb("blend_t", [P, 6, CH])
        taps = sb("taps", [P, CH // 4, 16])
        taps_half = sb("taps_half", [P, 2, CH // 4, 16], BF16)
        thr = sb("thr", [P, 2])
        omask = sb("omask", [P, 2, SUP])

        x_in = pair("x_in", [P, L])
        mid_out = pair("mid_out", [P, L])
        x_hi = sb("x_hi", [P, 4, BLK], BF16)
        x_lo = sb("x_lo", [P, 4, BLK], BF16)
        w_raw = pair("w_raw", [P, HID])
        w_hi = pair("w_hi", [P, HID], BF16)
        w_lo = pair("w_lo", [P, HID], BF16)
        batch_col = pair("batch_col", [P, 4])
        g32 = sb("g32", [P, 2, 2, BLK])
        g_hi = pair("g_hi", [P, 2, BLK], BF16, n=4)
        g_lo = pair("g_lo", [P, 2, BLK], BF16, n=4)
        tmask = pair("tmask", [P, BLK], n=4)
        mid_m = pair("mid_m", [P, BLK])

        SLOTS, GH = 4, 2
        xt = [x_in[s // 2][:, s % 2 * 1024:s % 2 * 1024 + 1024].rearrange(
            "p (g a t) -> p g a t", a=2, g=GH) for s in range(SLOTS)]
        toep = [mid_out[0][:, s * 512:s * 512 + 512].bitcast(BF16).rearrange(
            "p (g c t) -> p g c t", g=GH, c=2) for s in range(SLOTS)]
        u_hi = pair("u_hi", [P, 2, SUP], BF16, n=4)
        u_lo = pair("u_lo", [P, 2, SUP], BF16, n=4)
        b_hi = sb("b_hi", [P, 2, SUP], BF16)
        b_lo = sb("b_lo", [P, 2, SUP], BF16)
        s32 = pair("s32", [P, 2, SUP])
        s_hi = pair("s_hi", [P, 2, SUP], BF16)
        s_lo = pair("s_lo", [P, 2, SUP], BF16)
        e32 = pair("e32", [P, 2, 16, 16])
        e_hi = pair("e_hi", [P, 2, SUP], BF16, n=4)
        e_lo = pair("e_lo", [P, 2, SUP], BF16, n=4)
        etmp = pair("etmp", [P, 2, 16, 16])
        r_sb = pair("r_sb", [P, 2, P])
        r2_sb = pair("r2_sb", [P, 2, P])
        cols = pair("cols", [P, 6, GH])
        gain = sb("gain", [P, 2, P])
        gain_hi = pair("gain_hi", [P, 2, P], BF16)
        gain_lo = pair("gain_lo", [P, 2, P], BF16)
        y_m = [mid_m[i][:, :].rearrange("p (a t) -> p a t", a=2) for i in range(2)]
        o_sb = [g32[:, i, :, :].rearrange("p g (a t) -> p g a t", a=2) for i in range(2)]

        bank = [ctx.enter_context(nc.psum_tensor(f"bank{i}", [P, 512], F32)) for i in range(8)]
        hid_ps = [[bank[2 * i + h] for h in range(2)] for i in range(2)]
        mid_ps = [bank[4], bank[5]]
        up_ps = bank[0]
        bt_ps = bank[1]
        v_ps = [bank[2][:, :].rearrange("p (c k) -> p c k", c=2), bank[3][:, :].rearrange("p (c k) -> p c k", c=2)]
        y_ps = [bank[4], bank[5], bank[6], bank[7]]

        modes_in = sem("modes_in")
        params_in = sem("params_in")
        sid_in = sem("sid_in")
        consts = sem("consts")
        pool_step = sem("pool_step")
        dve_step = sem("dve_step")
        waves_in = sem("waves_in")
        waves = sem("waves")
        to_pe = sem("to_pe")
        pe_setup = sem("pe_setup")
        seeds_ready = sem("seeds_ready")
        l_ready = sem("l_ready")
        par_ready = sem("par_ready")
        x1_ready = sem("x1_ready")
        tables_ready = sem("tables_ready")
        taps_copied = sem("taps_copied")
        kernel_ready = sem("kernel_ready")
        kpad_out = sem("kpad_out")
        x_loaded = [[sem(f"x_loaded{i}_{j}") for j in range(NBLK)] for i in range(2)]
        w_loaded = [sem(f"w_loaded{i}") for i in range(2)]
        col_ready = sem("col_ready")
        w_high = sem("w_high")
        w_ready = sem("w_ready")
        x_high = sem("x_high")
        x_low = sem("x_low")
        mask_ready = sem("mask_ready")
        hid_ready = sem("hid_ready")
        gelu_done = sem("gelu_done")
        g_high = sem("g_high")
        g_low = sem("g_low")
        mid_ready = sem("mid_ready")
        mid_masked = sem("mid_masked")
        mid_added = sem("mid_added")
        mid_stored = [[sem(f"mid_stored{i}_{j}") for j in range(2)] for i in range(2)]
        xt_loaded = [sem(f"xt_loaded{i}") for i in range(SLOTS)]
        toep_loaded = [sem(f"toep_loaded{i}") for i in range(SLOTS)]
        u_turned = sem("u_turned")
        u_high = sem("u_high")
        u_low = sem("u_low")
        y_local = sem("y_local")
        y_done = sem("y_done")
        y_masked = sem("y_masked")
        o_ready = sem("o_ready")
        o_stored = [sem(f"o_stored{i}") for i in range(2)]
        b_made = sem("b_made")
        b_high = sem("b_high")
        b_low = sem("b_low")
        e_step = sem("e_step")
        e_ready = sem("e_ready")
        e_high = sem("e_high")
        e_low = sem("e_low")
        r_diag = sem("r_diag")
        r_ready = sem("r_ready")
        cols_ready = sem("cols_ready")
        gain_diag = sem("gain_diag")
        gain_ready = sem("gain_ready")
        gain_high = sem("gain_high")
        gain_low = sem("gain_low")
        v_done = sem("v_done")
        state_added = sem("state_added")
        state_first = sem("state_first")
        state_ready = sem("state_ready")
        s_high = sem("s_high")
        s_low = sem("s_low")

        block = ctx.enter_context(nc.Block())

        def wait(eng, s, value):
            if not isinstance(value, int) or value > 0:
                eng.wait_ge(s, value)

        def peeled(eng, count, body):
            body(0, True, False)
            with eng.Fori(1, count - 1) as i:
                body(i, False, False)
            body(count - 1, False, True)

        def pair_row(table, j, n, outer):
            v = table[:, :, bass.ds(j * GH, GH)].rearrange("p r g -> p g r")
            return v.unsqueeze(3).to_broadcast([P, GH, 16, n]) if outer else v.unsqueeze(2).to_broadcast([P, GH, n, 16])

        def w_count(b, s):
            return (b - s) * (16 // BPI) + 16

        def x_table(link, eng, rows, cols, tmp, s=None):
            n = rows.stop - rows.start
            row = lambda p: par_t[:, p, cols].unsqueeze(1).to_broadcast([P, n, cols.stop - cols.start])
            link(eng.tensor_tensor(tmp[0][:, 0:n, cols], l_re[:, rows, cols], row(ALPHA), ALU.mult), False)
            link(eng.tensor_tensor(tmp[1][:, 0:n, cols], l_im[:, rows, cols], row(BETA), ALU.mult))
            link(eng.tensor_tensor(x1[:, rows, cols], tmp[0][:, 0:n, cols], tmp[1][:, 0:n, cols], ALU.add), True, s)

        def powers(eng, j, q):
            wait(eng, e_low, j - 1)
            wait(eng, e_ready, j)
            eng.tensor_tensor(etmp[0][:, :, :, :], pair_row(l_re, j, 16, True), pair_row(z1, j, 16, False),
                              ALU.mult).then_inc(e_step, 1)
            eng.tensor_tensor(etmp[1][:, :, :, :], pair_row(l_im, j, 16, True), pair_row(z2, j, 16, False),
                              ALU.mult).then_inc(e_step, 1)
            eng.wait_ge(e_step, 2 * j + 2)
            eng.tensor_tensor(e32[q % 2][:, :, :, :], etmp[0][:, :, :, :], etmp[1][:, :, :, :],
                              ALU.add).then_inc(e_ready, 1)

        BPI = 2
        NI1 = B // BPI
        XCH = 3 * CH // 4
        AHEAD = 3
        HPI = SLOTS * GH
        NI2 = CH // HPI
        PPI = SLOTS
        KA = 1024 // SUP

        @block.sync
        def _(sp):
            for dst, src in (
                (expin[:, 0:MODES], log_a), (expin[:, MODES:MODES + 1], log_dt.rearrange("(p a) -> p a", a=1)),
                (aim[:, :], a_imag), (cc2[:, :, :], c_in),
            ):
                sp.dma_start(dst, src).then_inc(modes_in, 16)
            sp.dma_start(sid_row[:, :], sid.rearrange("(a n) -> a n", a=1)).then_inc(sid_in, 16)
            for dst, src in (
                (w2_raw[:, :, :], w2.rearrange("(a p) s -> p a s", p=P)),
                (b2_col[:, :], b2.rearrange("(p a) -> p a", a=1)), (bs_raw[:, :], b_sess),
                (sid8[:, :], sid.partition_broadcast(SESS)), (cc_i[:, :], chan_count.partition_broadcast(P)),
                (len_i[:, :], seq_len.partition_broadcast(P)),
            ):
                sp.dma_start(dst, src).then_inc(params_in, 16)
            for g in range(4):
                sp.dma_start(d_rows[32 * g:32 * g + 1, :],
                             d_in[g * 32:(g + 1) * 32].rearrange("(a n) -> a n", a=1)).then_inc(params_in, 16)
            for k in range(KA):
                sp.dma_start(olen_i[k * B:(k + 1) * B, :],
                             out_len.rearrange("(p a) -> p a", a=1)).then_inc(params_in, 16)

            sp.wait_ge(sid_in, 16)

            HALF = L // 2

            def load_block(b, s, q):
                cols = slice(q * BLK, (q + 1) * BLK)
                sp.dma_start(x_in[s][:, cols], x[bass.ds(b, 1), :, cols].rearrange("a c t -> (a c) t")
                             ).then_inc(x_loaded[s][q], 16)

            def load_weights(b, s):
                session = sp.value_load(sid_row[0:1, bass.ds(b, 1)], min_val=0, max_val=SESS - 1)
                sp.dma_start(w_raw[s][:, :], w_sess[bass.ds(session, 1), :, :].rearrange("a c h -> (a c) h")
                             ).then_inc(w_loaded[s], 16)

            for s in range(BPI):
                load_weights(s, s)
                for q in range(NBLK):
                    load_block(s, s, q)

            def store_kernel():
                sp.wait_ge(consts, 1)
                sp.dma_start(kpad_dram[:, :, 0:T - 1], zeros[:, :, 0:T - 1]).then_inc(kpad_out, 16)
                sp.wait_ge(kernel_ready, 1)
                for g in range(4):
                    for half in range(2):
                        sp.dma_start(bass.AP(tensor=kpad_dram.tensor, offset=(g * 32 * 2 + half) * KPAD + T - 1,
                                              ap=[[16, 16], [2 * KPAD, 32], [1, 16]]),
                                      taps_half[32 * g:32 * g + 16, half, :, :]).then_inc(kpad_out, 16)

            def store_and_load(i, first, last):
                for s in range(BPI):
                    b = i * BPI + s
                    if last and s == 0:
                        store_kernel()
                    if not last:
                        sp.wait_ge(w_ready, b + 1)
                        load_weights(b + BPI, s)
                    for q in range(NBLK):
                        sp.wait_ge(mid_added, NBLK * b + q + 1)
                        if not last:
                            load_block(b + BPI, s, q)
                        if q % 2 == 1:
                            half = q // 2
                            k0 = half * NSUP // 4
                            sp.dma_start(
                                mid_dram[k0:k0 + NSUP // 4, bass.ds(b, 1), :, :].rearrange("k a c t -> c (k a) t"),
                                mid_out[s][:, half * HALF:(half + 1) * HALF].rearrange("c (k t) -> c k t", t=2 * SUP)
                            ).then_inc(mid_stored[s][half], 16)
            peeled(sp, NI1, store_and_load)
            for s in range(BPI):
                for half in range(2):
                    sp.wait_ge(mid_stored[s][half], 16 * NI1)
            sp.wait_ge(kpad_out, 16 * 9)

            def load_group(g, s):
                src = bass.AP(tensor=mid_dram.tensor, offset=0,
                              ap=[[CH * 2 * SUP, P], [2 * SUP, CH], [1, 2 * SUP]])
                sp.dma_start(xt[s][:, :, :, :].rearrange("p g a t -> p g (a t)"),
                             src[:, bass.ds(g * GH, GH), :]).then_inc(xt_loaded[s], 16)
                src = bass.AP(tensor=kpad_dram.tensor, offset=0, ap=[[1, P], [KPAD, 2 * CH], [1, SUP]])
                sp.dma_start(toep[s][:, :, :, :].rearrange("p g c t -> p (g c) t"),
                             src[:, bass.ds(g * 2 * GH, 2 * GH), :]).then_inc(toep_loaded[s], 16)

            for s in range(SLOTS):
                load_group(s, s)

            def store_pairs(i, first, last):
                for q in range(PPI):
                    j = i * PPI + q
                    sp.wait_ge(o_ready, GH * j + GH)
                    for k in range(KA):
                        c0 = k * 2 * SUP
                        sp.dma_start(out[:, bass.ds(GH * j, GH), c0:c0 + 2 * SUP],
                                     o_sb[q % 2][k * B:(k + 1) * B, :, :, :].rearrange("b g a t -> b g (a t)")
                                     ).then_inc(o_stored[q % 2], 16)
                    if not last:
                        load_group((i + 1) * SLOTS + q, q)
            peeled(sp, NI2, store_pairs)
            for s in range(2):
                sp.wait_ge(o_stored[s], 16 * KA * CH // GH // 2)

        @block.gpsimd
        def _(pool):
            steps = [0]

            def link(ins, waits=True, s=None):
                steps[0] += 1
                ins.then_inc(pool_step, 1)
                if waits:
                    pool.wait_ge(pool_step, steps[0])

            for m in (ident[:, :], swap[:, :], zeros[:, :, :], taps[:, :, :]):
                link(pool.memset(m, 0.0))
            for m, off in ((ident, 0), (swap, MODES), (swap, -MODES)):
                link(pool.affine_select(out=m[:, :], in_=m[:, :], compare_op=ALU.not_equal, fill=1.0,
                                        base=off, pattern=[[-1, P]], channel_multiplier=1))
            link(pool.iota(part[:, :], [[0, 1]], base=0, channel_multiplier=1,
                           allow_small_or_imprecise_dtypes=True))
            link(pool.iota(time_row[:, :], [[1, L]], base=0, channel_multiplier=0,
                           allow_small_or_imprecise_dtypes=True))
            link(pool.memset(sgn[0:MODES, :], -1.0))
            link(pool.memset(sgn[MODES:P, :], 1.0))
            for k in range(KA):
                link(pool.memset(thr[k * B:(k + 1) * B, 0:1], float(-2 * k * SUP)))
                link(pool.memset(thr[k * B:(k + 1) * B, 1:2], float(-(2 * k + 1) * SUP)))
            for m in s32:
                link(pool.memset(m[:, :, 0:B], 0.0))
            pool.drain().then_inc(consts, 1)

            pool.wait_ge(seeds_ready, 1)
            re, im = l_re, l_im
            tmp = [g32[:, k, :, :].rearrange("p h (r c) -> p (h r) c", c=CH) for k in range(2)]
            link(pool.memset(re[:, 0, :], 1.0), False)
            link(pool.memset(im[:, 0, :], 0.0), False)
            link(pool.tensor_copy(re[:, 1, :], seed_re[:, 1, :]), False)
            link(pool.tensor_copy(im[:, 1, :], seed_im[:, 1, :]))
            for n, m in ((1, 1), (2, 2), (4, 4), (8, 7)):
                top_re = re[:, n, :].unsqueeze(1).to_broadcast([P, m, CH])
                top_im = im[:, n, :].unsqueeze(1).to_broadcast([P, m, CH])
                low, new, t = slice(1, m + 1), slice(n + 1, n + m + 1), slice(0, m)
                for dst, a, b, op in ((re, top_re, top_im, ALU.subtract), (im, top_im, top_re, ALU.add)):
                    link(pool.tensor_tensor(tmp[0][:, t, :], re[:, low, :], a, ALU.mult), False)
                    link(pool.tensor_tensor(tmp[1][:, t, :], im[:, low, :], b, ALU.mult))
                    link(pool.tensor_tensor(dst[:, new, :], tmp[0][:, t, :], tmp[1][:, t, :], op))
            pool.drain().then_inc(l_ready, 1)
            pool.wait_ge(par_ready, 1)
            for rows in (slice(0, 8), slice(8, 16)):
                x_table(link, pool, rows, slice(XCH, CH), tmp)
            pool.drain().then_inc(x1_ready, 1)

            def low_half(i, u):
                n, s, q = i * BPI * NBLK + u, u // NBLK % BPI, u % NBLK
                pool.wait_ge(x_high, n + 1)
                pool.tensor_tensor(x_lo[:, q, :], x_in[s][:, q * BLK:(q + 1) * BLK], x_hi[:, q, :],
                                   ALU.subtract).then_inc(x_low, 1)

            def add_x(i, u):
                n, s, q = i * BPI * NBLK + u, u // NBLK % BPI, u % NBLK
                cols = slice(q * BLK, (q + 1) * BLK)
                pool.wait_ge(mid_masked, n + 1)
                if q % 2 == 0:
                    wait(pool, mid_stored[s][q // 2], 16 * i)
                pool.tensor_tensor(
                    mid_out[s][:, cols].rearrange("p (c t) -> p c t", t=T)[:, :, T - 1::-1],
                    mid_m[u % 2][:, :].rearrange("p (c t) -> p c t", t=T),
                    x_in[s][:, cols].rearrange("p (c t) -> p c t", t=T), ALU.add).then_inc(mid_added, 1)

            for u in range(AHEAD):
                low_half(0, u)

            def blocks_pool(i, first, last):
                for u in range(BPI * NBLK):
                    if not (last and u >= BPI * NBLK - AHEAD):
                        low_half(i, u + AHEAD)
                    if not (first and u < 2):
                        add_x(i - 1 if u < 2 else i, (u - 2) % (BPI * NBLK))
            peeled(pool, NI1, blocks_pool)
            for u in (-2, -1):
                add_x(NI1 - 1, BPI * NBLK + u)

            def state_low(j, q):
                pool.wait_ge(s_high, j + 1)
                pool.tensor_tensor(s_lo[q % 2][:, :, :], s32[q % 2][:, :, :], s_hi[q % 2][:, :, :],
                                   ALU.subtract).then_inc(s_low, 1)

            def add_input(h, u):
                s, g = u // GH, u % GH
                pool.wait_ge(y_masked, h + 1)
                if g == 0:
                    wait(pool, o_stored[s % 2], (h - u % (2 * GH)) // (2 * GH) * (16 * KA) if isinstance(h, int)
                         else (h - u % (2 * GH)) * (16 * KA // (2 * GH)))
                pool.tensor_tensor(
                    o_sb[s % 2][:, g, :, :].rearrange("p a (c t) -> p a c t", t=T),
                    y_m[u % 2].rearrange("p a (c t) -> p a c t", t=T),
                    xt[s][:, g, :, :].rearrange("p a (c t) -> p a c t", t=T)[:, :, :, T - 1::-1],
                    ALU.add).then_inc(o_ready, 1)

            pool.wait_ge(tables_ready, 1)
            powers(pool, 1, 1)

            def pairs_pool(i, first, last):
                for q in range(PPI):
                    j = i * PPI + q
                    start = first and q == 0
                    if not start:
                        state_low(j - 1, q + 1)
                    if not (last and q >= PPI - 2):
                        powers(pool, j + 2, q + 2)
                    if not start:
                        for g in range(GH):
                            add_input(GH * (j - 1) + g, (GH * (q - 1) + g) % HPI)
            peeled(pool, NI2, pairs_pool)
            state_low(CH // GH - 1, PPI - 1)
            for g in range(GH):
                add_input(CH - GH + g, HPI - GH + g)

        @block.scalar
        def _(act):
            act.wait_ge(waves_in, 1)
            act.activation(hv[4][:, :], hv[2][:, :], ACT.Sin, scale=TWO_PI).then_inc(waves, 1)
            act.activation(hv[5][:, :], hv[2][:, :], ACT.Sin, scale=TWO_PI / 2).then_inc(waves, 1)
            act.activation(hv[6][:, :], par[:, RHO, 0, :], ACT.Tanh, scale=-0.5).then_inc(waves, 1)
            act.wait_ge(waves_in, 2)
            act.activation(seed[:, :, :], seed[:, :, :], ACT.Tanh, scale=-0.5).then_inc(waves, 1)
            act.wait_ge(waves_in, 4)
            act.activation(seed_im[:, :, :], seed_im[:, :, :], ACT.Sin, scale=TWO_PI).then_inc(waves, 1)
            act.activation(seed_re[:, :, :], seed_re[:, :, :], ACT.Sin, scale=TWO_PI).then_inc(waves, 1)
            def weights_high(b, s):
                act.wait_ge(w_loaded[s], w_count(b, s))
                act.wait_ge(col_ready, b + 1)
                wait(act, hid_ready, 2 * NBLK * (b - 1))
                act.activation(w_hi[s][:, :], w_raw[s][:, :], ACT.Copy, scale=batch_col[s][:, 0:1]).then_inc(w_high, 1)

            weights_high(0, 0)

            def copy_taps(g):
                act.wait_ge(pe_setup, 4)
                rows = slice(32 * g, 32 * g + 16)
                act.activation(taps[rows, :, :], bank[7][rows, :].rearrange("p (h r) -> p h r", r=16), ACT.Copy
                               ).then_inc(taps_copied, 1)

            def gelus(i, first, last):
                for u in range(BPI * NBLK):
                    n = i * BPI * NBLK + u
                    wait(act, g_low, n - 1)
                    for h in range(2):
                        act.wait_ge(hid_ready, 2 * n + h + 1)
                        act.activation(g32[:, u % 2, h, :], hid_ps[u % 2][h][:, :], ACT.Gelu,
                                       bias=batch_col[u // NBLK][:, 2 + h:3 + h]
                                       ).then_inc(gelu_done, 1)
                    act.wait_ge(gelu_done, 2 * n + 2)
                    wait(act, mid_ready, n - 3)
                    act.activation(g_hi[u % 4][:, :, :], g32[:, u % 2, :, :], ACT.Copy).then_inc(g_high, 1)
                    if u % NBLK == 1 and not (last and u > NBLK):
                        weights_high(i * BPI + u // NBLK + 1, (u // NBLK + 1) % BPI)
                    if first and u >= NBLK:
                        copy_taps(u - NBLK)
            peeled(act, NI1, gelus)

            def high(dst, src, s):
                act.activation(dst, src, ACT.Copy).then_inc(s, 1)

            def state_high(j, q):
                act.wait_ge(state_ready, 4 * j + 4)
                wait(act, y_done, GH * (j - 1))
                high(s_hi[q % 2][:, :, :], s32[q % 2][:, :, :], s_high)

            def input_high(h, u):
                act.wait_ge(u_turned, h + 1)
                wait(act, y_local, h - 3)
                high(u_hi[u % 4][:, :, :], up_ps[:, :].rearrange("p (c k) -> p c k", c=2), u_high)

            def matrix_high(j):
                act.wait_ge(b_made, j + 1)
                wait(act, v_done, j)
                high(b_hi[:, :, :], bt_ps[:, :].rearrange("p (g c) -> p g c", g=GH), b_high)

            def powers_high(j, q):
                act.wait_ge(e_ready, j + 1)
                wait(act, y_done, GH * (j - 3))
                high(e_hi[q % 4][:, :, :], e32[q % 2][:, :, :, :].rearrange("p g a b -> p g (a b)"), e_high)

            def diagonals(dst, k, q, s):
                for g in range(GH):
                    act.activation(dst[:, g, :], ident[:, :], ACT.Copy, scale=cols[q % 2][:, k, g:g + 1]).then_inc(s, 1)

            def gain_diagonals(j, q):
                act.wait_ge(cols_ready, j + 1)
                wait(act, gain_low, j)
                diagonals(gain, 0, q, gain_diag)

            def gains_high(j, q):
                act.wait_ge(gain_ready, GH * j + GH)
                wait(act, b_made, j - 1)
                high(gain_hi[q % 2][:, :, :], gain[:, :, :], gain_high)

            def step_diagonals(j, q, k):
                if k == 2:
                    wait(act, state_added, 4 * (j - 1))
                    act.wait_ge(cols_ready, j + 1)
                diagonals((r_sb if k == 2 else r2_sb)[q % 2], k, q, r_diag)

            def halves(i, first, last):
                for q in range(PPI):
                    j = i * PPI + q
                    end, end2 = last and q == PPI - 1, last and q >= PPI - 2
                    if not end:
                        gains_high(j + 1, q + 1)
                        step_diagonals(j + 1, q + 1, 2)
                        input_high(GH * (j + 1), GH * (q + 1))
                    if not end2:
                        gain_diagonals(j + 2, q + 2)
                    if not end:
                        matrix_high(j + 1)
                        input_high(GH * (j + 1) + 1, GH * (q + 1) + 1)
                        step_diagonals(j + 1, q + 1, 4)
                    state_high(j, q)
                    if not end2:
                        powers_high(j + 2, q + 2)
            gain_diagonals(0, 0)
            powers_high(0, 0)
            gains_high(0, 0)
            for k in (2, 4):
                step_diagonals(0, 0, k)
            matrix_high(0)
            for g in range(GH):
                input_high(g, g)
            gain_diagonals(1, 1)
            powers_high(1, 1)
            peeled(act, NI2, halves)

        @block.vector
        def _(dve):
            done = {}

            def link(ins, waits=True, s=None):
                s = s or dve_step
                done[s.name] = done.get(s.name, 0) + 1
                ins.then_inc(s, 1)
                if waits:
                    dve.wait_ge(s, done[s.name])

            def ts(o, i, a, op0, b=None, op1=ALU.bypass, waits=True, s=None):
                if b is None:
                    link(dve.tensor_scalar(o, i, a, None, op0), waits, s)
                else:
                    link(dve.tensor_scalar(o, i, a, b, op0, op1), waits, s)

            def tt(o, a, b, op, waits=True, s=None):
                link(dve.tensor_tensor(o, a, b, op), waits, s)

            def stt(o, a, c, op0, b, op1, waits=True, s=None):
                link(dve.scalar_tensor_tensor(o, a, c, b, op0, op1), waits, s)

            def copy(o, i, waits=True, s=None):
                link(dve.tensor_copy(o, i), waits, s)

            dve.wait_ge(modes_in, 16 * 4)
            n_, r_, q_, y_ = (e[:, :] for e in ex)
            ts(n_, expin[:, :], LOG2E, ALU.mult, ROUND, ALU.add)
            ts(n_, n_, ROUND, ALU.subtract)
            ts(n_, n_, -126.0, ALU.max, 127.0, ALU.min)
            stt(r_, n_, -LN2_HI, ALU.mult, expin[:, :], ALU.add)
            stt(r_, n_, -LN2_LO, ALU.mult, r_, ALU.add)
            ts(ex_i[:, :], n_, 127.0, ALU.add, 2.0 ** 23, ALU.mult, waits=False)
            ts(q_, r_, 1.0 / 5040, ALU.mult)
            for k in (720, 120, 24, 6, 2, 1):
                stt(q_, q_, 1.0 / k, ALU.add, r_, ALU.mult)
            stt(y_, q_, 1.0, ALU.add, ex_i[:, :].bitcast(F32), ALU.mult)
            ar, dt = ex[3][:, 0:MODES], ex[3][:, MODES:MODES + 1]

            h_ = [m[:, :] for m in hv]
            for a in range(2):
                ts(par[:, F, a, :], aim[:, :], dt, ALU.mult, 1.0 / (2 * math.pi), ALU.mult, waits=False)
                ts(par[:, RHO, a, :], ar, dt, ALU.mult, s=to_pe if a == 1 else None)
            f = par[:, F, 0, :]
            ts(h_[3], f, ROUND, ALU.add)
            ts(h_[3], h_[3], ROUND, ALU.subtract)
            tt(h_[2], f, h_[3], ALU.subtract, s=waves_in)

            dve.wait_ge(params_in, 16 * (6 + 4 + KA))
            dve.wait_ge(consts, 1)
            copy(onehot[:, :], sid8[:, :], waits=False)
            copy(ccf[:, :], cc_i[:, :], waits=False)
            copy(batch_t[:, :, 1], len_i[:, :], waits=False)
            copy(w2hi[:, :, :], w2_raw[:, :, :], waits=False)
            copy(blend_t[:, 0, 0:1], olen_i[:, :])
            ts(onehot[:, :], onehot[:, :], part[0:SESS, :], ALU.is_equal, s=to_pe)
            ts(batch_t[:, :, 0], ccf[:, :], part[:, :], ALU.is_gt, waits=False)
            tt(w2lo[:, :, :], w2_raw[:, :, :], w2hi[:, :, :], ALU.subtract, waits=False)
            ts(thr[:, :], thr[:, :], blend_t[:, 0, 0:1], ALU.add)
            for a in range(2):
                ts(omask[:, a, :], time_row[:, 0:SUP], thr[:, a:a + 1], ALU.is_lt, waits=False)

            dve.wait_ge(pe_setup, 1)
            copy(par_t[:, 0:2, :], bank[5][:, 0:2 * CH].rearrange("p (c h) -> p c h", c=2))
            turns, whole = (m[:, :, :] for m in seed_t)
            for k, r in enumerate(POWERS):
                ts(seed[:, k, :], par_t[:, RHO, :], r, ALU.mult, waits=False)
                ts(turns[:, k, :], par_t[:, F, :], r, ALU.mult, waits=k == NPOW - 1)
            dve.drain().then_inc(waves_in, 1)
            for dst in (seed_im, seed_re):
                ts(whole, turns, ROUND, ALU.add)
                ts(whole, whole, ROUND, ALU.subtract)
                tt(dst[:, :, :], turns, whole, ALU.subtract, s=waves_in)
                if dst is seed_im:
                    ts(turns, turns, 0.25, ALU.add)
            tt(h_[7], ar, ar, ALU.mult, waits=False)
            tt(h_[8], aim[:, :], aim[:, :], ALU.mult)
            tt(h_[7], h_[7], h_[8], ALU.add)
            link(dve.reciprocal(h_[7], h_[7]))
            dve.wait_ge(waves, 4)
            ts(whole, seed[:, :, :], -1.0, ALU.mult, 1.0, ALU.add)
            link(dve.reciprocal(whole, whole))
            stt(seed[:, :, :], seed[:, :, :], 1.0, ALU.add, whole, ALU.mult)
            dve.wait_ge(waves, 6)
            tt(seed_im[:, :, :], seed_im[:, :, :], seed[:, :, :], ALU.mult, waits=False)
            tt(seed_re[:, :, :], seed_re[:, :, :], seed[:, :, :], ALU.mult)
            dve.drain().then_inc(seeds_ready, 1)

            stt(h_[5], h_[5], -2.0, ALU.mult, h_[5], ALU.mult, waits=False)
            ts(h_[8], h_[6], -1.0, ALU.mult, 1.0, ALU.add)
            link(dve.reciprocal(h_[8], h_[8]))
            stt(h_[6], h_[6], 2.0, ALU.mult, h_[8], ALU.mult)
            stt(h_[9], h_[6], 1.0, ALU.add, h_[4], ALU.mult, waits=False)
            stt(h_[8], h_[5], 1.0, ALU.add, h_[6], ALU.mult)
            tt(h_[8], h_[8], h_[5], ALU.add)
            tt(h_[0], h_[8], ar, ALU.mult, waits=False)
            tt(h_[1], h_[9], aim[:, :], ALU.mult, waits=False)
            tt(h_[2], h_[8], aim[:, :], ALU.mult, waits=False)
            tt(h_[3], h_[9], ar, ALU.mult)
            tt(h_[10], h_[1], h_[0], ALU.subtract, waits=False)
            stt(h_[11], h_[2], -1.0, ALU.mult, h_[3], ALU.subtract)
            tt(h_[10], h_[10], h_[7], ALU.mult, waits=False)
            tt(h_[11], h_[11], h_[7], ALU.mult)
            cr, ci = cc2[:, :, 0], cc2[:, :, 1]
            tt(h_[0], h_[10], cr, ALU.mult, waits=False)
            tt(h_[1], h_[11], ci, ALU.mult, waits=False)
            tt(h_[4], h_[11], cr, ALU.mult, waits=False)
            tt(h_[5], h_[10], ci, ALU.mult)
            ts(h_[8], h_[8], 1.0, ALU.add, waits=False)
            tt(h_[2], h_[0], h_[1], ALU.subtract, waits=False)
            tt(h_[3], h_[4], h_[5], ALU.add)
            tt(h_[0], h_[2], h_[8], ALU.mult, waits=False)
            tt(h_[1], h_[3], h_[9], ALU.mult, waits=False)
            tt(h_[4], h_[2], h_[9], ALU.mult, waits=False)
            tt(h_[5], h_[3], h_[8], ALU.mult)
            tt(h_[6], h_[0], h_[1], ALU.subtract, waits=False)
            tt(h_[7], h_[4], h_[5], ALU.add)
            for k, a, row, factor in ((ALPHA, 0, 2, 2.0), (ALPHA, 1, 3, -2.0), (BETA, 0, 3, -2.0), (BETA, 1, 2, -2.0),
                                      (GAIN_D, 0, 6, 2.0), (GAIN_D, 1, 6, -2.0), (GAIN_O, 0, 7, -2.0), (GAIN_O, 1, 7, -2.0)):
                ts(par[:, k, a, :], h_[row], factor, ALU.mult, waits=False)
            dve.drain().then_inc(to_pe, 1)

            sq_re, sq_im = (e32[k][:, :, :, :].rearrange("p g a b -> p (g a b)").rearrange("p (k h) -> p k h", h=CH)
                            for k in range(2))
            tmp = [m[:, :].rearrange("p (r h) -> p r h", h=CH) for m in mid_out]
            copy(sq_re[:, 0, :], seed_re[:, 0, :], waits=False)
            copy(sq_im[:, 0, :], seed_im[:, 0, :])

            def squared(re_out, im_out, re, im):
                tt(tmp[0][:, 0, :], re, re, ALU.mult, waits=False)
                tt(tmp[1][:, 0, :], im, im, ALU.mult, waits=False)
                stt(im_out, re, 2.0, ALU.mult, im, ALU.mult)
                tt(re_out, tmp[0][:, 0, :], tmp[1][:, 0, :], ALU.subtract)
            for k in range(3):
                squared(sq_re[:, k + 1, :], sq_im[:, k + 1, :], sq_re[:, k, :], sq_im[:, k, :])
            top, low = slice(0, MODES), slice(MODES, P)
            for z, one, none in ((z1, top, low), (z2, low, top)):
                link(dve.memset(z[one, 0, :], 1.0), False)
                link(dve.memset(z[none, 0, :], 0.0))
            for k in range(4):
                n = 1 << k
                re_n = sq_re[:, k, :].unsqueeze(1).to_broadcast([P, n, CH])
                im_n = sq_im[:, k, :].unsqueeze(1).to_broadcast([P, n, CH])
                old, new = slice(0, n), slice(n, 2 * n)
                for dst, a, b, op in ((z1, z1, z2, ALU.add), (z2, z2, z1, ALU.subtract)):
                    tt(tmp[0][:, old, :], a[:, old, :], re_n, ALU.mult, waits=False)
                    tt(tmp[1][:, old, :], b[:, old, :], im_n, ALU.mult)
                    tt(dst[:, new, :], tmp[0][:, old, :], tmp[1][:, old, :], op)
            dve.wait_ge(pe_setup, 2)
            copy(batch_t[:, :, 2:4], bank[7][:, 0:2 * B].rearrange("p (c b) -> p b c", c=2), waits=False)
            dve.wait_ge(pe_setup, 3)
            copy(par_t[:, 2:NPAR, :], bank[6][:, :].rearrange("p (c h) -> p c h", c=4), s=par_ready)
            copy(blend_t[:, 0:2, :], par_t[:, GAIN_D:GAIN_O + 1, :], waits=False)
            copy(blend_t[:, 2, :], seed_re[:, 2, :], waits=False)
            squared(blend_t[:, 4, :], blend_t[:, 5, :], seed_re[:, 2, :], seed_im[:, 2, :])
            ts(blend_t[:, 3, :], seed_im[:, 2, :], sgn[:, :], ALU.mult, waits=False)
            ts(blend_t[:, 5, :], blend_t[:, 5, :], sgn[:, :], ALU.mult)
            dve.wait_ge(l_ready, 1)
            x_table(link, dve, slice(0, 16), slice(0, XCH), tmp, to_pe)

            def kernel_taps(g):
                dve.wait_ge(taps_copied, g + 1)
                one = slice(32 * g, 32 * g + 1)
                tt(taps[one, :, 0], taps[one, :, 0], d_rows[one, :], ALU.add)
                if g == 3:
                    link(dve.tensor_copy(taps_half[:, 0, :, :], taps[:, :, :]))
                    tt(taps_half[:, 1, :, :], taps[:, :, :], taps_half[:, 0, :, :], ALU.subtract, s=kernel_ready)
                    dve.drain().then_inc(tables_ready, 1)

            def batch_columns(b, s):
                wait(dve, mask_ready, NBLK * (b - 1))
                dve.tensor_copy(batch_col[s][:, :], batch_t[:, bass.ds(b, 1), :].rearrange("p a c -> p (a c)")
                                ).then_inc(col_ready, 1)

            def weights_low(b, s):
                dve.wait_ge(w_high, b + 1)
                dve.scalar_tensor_tensor(w_lo[s][:, :], w_raw[s][:, :], batch_col[s][:, 0:1], w_hi[s][:, :],
                                         ALU.mult, ALU.subtract).then_inc(w_ready, 1)

            def high_half(i, u):
                n, s, q = i * BPI * NBLK + u, u // NBLK % BPI, u % NBLK
                dve.wait_ge(x_loaded[s][q], 16 * i + 16 + 16 * (u // (BPI * NBLK)))
                wait(dve, hid_ready, 2 * n - 6)
                dve.tensor_copy(x_hi[:, q, :], x_in[s][:, q * BLK:(q + 1) * BLK]).then_inc(x_high, 1)

            def time_mask(n, u):
                cols = slice(u % NBLK * BLK, (u % NBLK + 1) * BLK)
                wait(dve, mid_masked, n - 3)
                dve.tensor_scalar(tmask[u % 4][:, :], time_row[:, cols], batch_col[u // NBLK][:, 1:2], None,
                                  ALU.is_lt).then_inc(mask_ready, 1)

            def mask_block(n, u):
                dve.wait_ge(mid_ready, n + 1)
                dve.wait_ge(mask_ready, n + 1)
                wait(dve, mid_added, n - 1)
                dve.scalar_tensor_tensor(mid_m[u % 2][:, :], mid_ps[u % 2][:, :], b2_col[:, :], tmask[u % 4][:, :],
                                         ALU.add, ALU.mult).then_inc(mid_masked, 1)

            def blocks(i, first, last):
                for u in range(BPI * NBLK):
                    n, b = i * BPI * NBLK + u, i * BPI + u // NBLK
                    next_batch = (b + 1, (u // NBLK + 1) % BPI)
                    dve.wait_ge(g_high, n + 1)
                    wait(dve, mid_ready, n - 3)
                    dve.tensor_tensor(g_lo[u % 4][:, :, :], g32[:, u % 2, :, :], g_hi[u % 4][:, :, :],
                                      ALU.subtract).then_inc(g_low, 1)
                    if u % NBLK == 0 and not (last and u >= NBLK):
                        batch_columns(*next_batch)
                    if not (first and u < 2):
                        mask_block(n - 2, (u - 2) % (BPI * NBLK))
                    time_mask(n, u)
                    if not (last and u >= BPI * NBLK - AHEAD):
                        high_half(i, u + AHEAD)
                    if u % NBLK == 1 and not (last and u >= NBLK):
                        weights_low(*next_batch)
                    if first and u >= NBLK:
                        kernel_taps(u - NBLK)
            batch_columns(0, 0)
            high_half(0, 0)
            weights_low(0, 0)
            for u in range(1, AHEAD):
                high_half(0, u)
            peeled(dve, NI1, blocks)
            for u in (-2, -1):
                mask_block(B * NBLK + u, BPI * NBLK + u)

            def columns(j, q):
                wait(dve, r_ready, 2 * GH * (j - 1))
                dve.tensor_copy(cols[q % 2][:, :, :], blend_t[:, :, bass.ds(GH * j, GH)]).then_inc(cols_ready, 1)

            def off_diagonals(dst, k, q, s):
                for g in range(GH):
                    dve.scalar_tensor_tensor(dst[:, g, :], swap[:, :], cols[q % 2][:, k + 1, g:g + 1], dst[:, g, :],
                                             ALU.mult, ALU.add).then_inc(s, 1)

            def gains(j, q):
                dve.wait_ge(gain_diag, GH * j + GH)
                off_diagonals(gain, 0, q, gain_ready)

            def gains_low(j, q):
                dve.wait_ge(gain_high, j + 1)
                dve.tensor_tensor(gain_lo[q % 2][:, :, :], gain[:, :, :], gain_hi[q % 2][:, :, :],
                                  ALU.subtract).then_inc(gain_low, 1)

            def transition(j, q, k):
                dve.wait_ge(r_diag, 2 * GH * j + k // 2 * GH)
                off_diagonals((r_sb if k == 2 else r2_sb)[q % 2], k, q, r_ready)

            def keep_states(k, j, q):
                if k == 0:
                    dve.wait_ge(v_done, j + 1)
                    wait(dve, s_low, j - 1)
                    dst, src, n = 4, 0, 3
                else:
                    dve.wait_ge(state_added, 4 * j + k)
                    dst, src, n = (k, 3 + k, 1) if k < 4 else (5, 1, 3)
                dve.tensor_copy(s32[q % 2][:, :, dst * B:(dst + n) * B],
                                v_ps[q % 2][:, :, src * B:(src + n) * B]
                                ).then_inc(state_first if k == 0 else state_ready, 1)

            def input_low(h, u):
                dve.wait_ge(u_high, h + 1)
                dve.tensor_tensor(u_lo[u % 4][:, :, :], up_ps[:, :].rearrange("p (c k) -> p c k", c=2),
                                  u_hi[u % 4][:, :, :], ALU.subtract).then_inc(u_low, 1)

            def matrix_low(j):
                dve.wait_ge(b_high, j + 1)
                dve.tensor_tensor(b_lo[:, :, :], bt_ps[:, :].rearrange("p (g c) -> p g c", g=GH), b_hi[:, :, :],
                                  ALU.subtract).then_inc(b_low, 1)

            def powers_low(j, q):
                dve.wait_ge(e_high, j + 1)
                dve.tensor_tensor(e_lo[q % 4][:, :, :], e32[q % 2][:, :, :, :].rearrange("p g a b -> p g (a b)"),
                                  e_hi[q % 4][:, :, :], ALU.subtract).then_inc(e_low, 1)

            def mask_output(h, u):
                dve.wait_ge(y_done, h + 1)
                wait(dve, o_ready, h - 1)
                dve.tensor_tensor(y_m[u % 2], y_ps[u % 4][:, :].rearrange("p (a t) -> p a t", a=2),
                                  omask[:, :, :], ALU.mult).then_inc(y_masked, 1)

            powers(dve, 0, 0)
            columns(0, 0)
            columns(1, 1)
            gains(0, 0)
            powers_low(0, 0)
            gains_low(0, 0)
            transition(0, 0, 2)
            transition(0, 0, 4)
            matrix_low(0)
            input_low(0, 0)
            input_low(1, 1)
            keep_states(0, 0, 0)
            gains(1, 1)
            powers_low(1, 1)

            def pairs_dve(i, first, last):
                for q in range(PPI):
                    j = i * PPI + q
                    start, end, end2 = first and q == 0, last and q == PPI - 1, last and q >= PPI - 2
                    h, u = GH * j, GH * q
                    keep_states(1, j, q)
                    if not end:
                        gains_low(j + 1, q + 1)
                    if not end2:
                        columns(j + 2, q + 2)
                    if not end:
                        transition(j + 1, q + 1, 2)
                    keep_states(2, j, q)
                    if not end:
                        input_low(h + 2, u + 2)
                    keep_states(3, j, q)
                    if not end:
                        matrix_low(j + 1)
                        input_low(h + 3, u + 3)
                    keep_states(4, j, q)
                    if not start:
                        mask_output(h - 2, u + 2)
                    if not end:
                        transition(j + 1, q + 1, 4)
                    if not end2:
                        gains(j + 2, q + 2)
                    if not end:
                        keep_states(0, j + 1, q + 1)
                    if not start:
                        mask_output(h - 1, u + 3)
                    if not end2:
                        powers_low(j + 2, q + 2)
            peeled(dve, NI2, pairs_dve)
            for g in range(GH):
                mask_output(CH - GH + g, HPI - GH + g)

        @block.tensor
        def _(pe):
            def turn_rows(bank_, rows):
                for at, k in enumerate(rows):
                    ins = pe.transpose(bank_[:, at * CH:(at + 1) * CH], par[:, k, :, :].rearrange("p a m -> p (a m)"),
                                       ident[:, :])
                ins.then_inc(pe_setup, 1)
            pe.wait_ge(consts, 1)
            pe.wait_ge(to_pe, 1)
            turn_rows(bank[5], (F, RHO))
            pe.wait_ge(to_pe, 2)
            for h in range(2):
                ins = pe.matmul(bank[7][:, h * B:(h + 1) * B], bs_raw[:, h * P:(h + 1) * P], onehot[:, :],
                                start=True, stop=True)
            ins.then_inc(pe_setup, 1)
            pe.wait_ge(to_pe, 3)
            turn_rows(bank[6], (ALPHA, BETA, GAIN_D, GAIN_O))

            def kernel_products():
                pe.wait_ge(to_pe, 4)
                pe.wait_ge(x1_ready, 1)
                for h in range(CH):
                    g, c = h // 32, h % 32 * 16
                    ins = pe.matmul(bank[7][32 * g:32 * g + 16, c:c + 16], x1[:, :, h], z1[:, :, h],
                                    start=True, stop=True)
                ins.then_inc(pe_setup, 1)

            def keep_clock(o, data, n):
                for _ in range(n):
                    pe.matmul(o, w2hi[:, 0, :], data, start=True, stop=True)

            pe.wait_ge(l_ready, 1)
            keep_clock(bank[5][:, 0:2 * CH], w2hi[:, :, :].rearrange("p a c -> p (a c)"), 40)

            def hidden(i, n, u):
                s, q = u // NBLK, u % NBLK
                pe.wait_ge(x_low, n + 1)
                if q == 0:
                    pe.wait_ge(w_ready, i * BPI + s + 1)
                for h in range(2):
                    wait(pe, gelu_done, 2 * n - 3 + h)
                    cols = slice(h * P, (h + 1) * P)
                    o = hid_ps[u % 2][h][:, :]
                    pe.matmul(o, w_hi[s][:, cols], x_hi[:, q, :], start=True, stop=False)
                    pe.matmul(o, w_hi[s][:, cols], x_lo[:, q, :], start=False, stop=False)
                    pe.matmul(o, w_lo[s][:, cols], x_hi[:, q, :], start=False, stop=True).then_inc(hid_ready, 1)

            def project(n, u):
                pe.wait_ge(g_low, n + 1)
                wait(pe, mid_masked, n - 1)
                o = mid_ps[u % 2][:, :]
                for h in range(2):
                    pe.matmul(o, w2hi[:, h, :], g_hi[u % 4][:, h, :], start=h == 0, stop=False)
                    pe.matmul(o, w2lo[:, h, :], g_hi[u % 4][:, h, :], start=False, stop=False)
                    ins = pe.matmul(o, w2hi[:, h, :], g_lo[u % 4][:, h, :], start=False, stop=h == 1)
                ins.then_inc(mid_ready, 1)

            def blocks_pe(i, first, last):
                for u in range(BPI * NBLK):
                    n = i * BPI * NBLK + u
                    hidden(i, n, u)
                    if first and u == 1:
                        kernel_products()
                    if not (first and u < 2):
                        project(n - 2, (u - 2) % (BPI * NBLK))
            peeled(pe, NI1, blocks_pe)
            for u in (-2, -1):
                project(B * NBLK + u, BPI * NBLK + u)

            def three(out_, left_hi, left_lo, right_hi, right_lo, start, stop, skip=False):
                pe.matmul(out_, left_hi, right_hi, start=start, stop=False, skip_group_check=skip)
                pe.matmul(out_, left_hi, right_lo, start=False, stop=False, skip_group_check=skip)
                return pe.matmul(out_, left_lo, right_hi, start=False, stop=stop, skip_group_check=skip)

            def turn(i, h, u):
                s, g = u // GH, u % GH
                if g == 0:
                    pe.wait_ge(xt_loaded[s], 16 * i + 16)
                wait(pe, u_low, h)
                for c in range(2):
                    for a in range(2):
                        o = (c * 2 + a) * P
                        ins = pe.transpose(up_ps[:, o:o + P], xt[s][:, g, a, c * T:(c + 1) * T], ident[:, :])
                ins.then_inc(u_turned, 1)

            def input_matrices(j, q):
                pe.wait_ge(e_low, j + 1)
                pe.wait_ge(gain_low, j + 1)
                wait(pe, b_low, j)
                for g in range(GH):
                    for c in range(2):
                        o, t = g * SUP + c * P, slice(c * T, (c + 1) * T)
                        ins = three(bt_ps[:, o:o + P], e_hi[q % 4][:, g, t], e_lo[q % 4][:, g, t],
                                    gain_hi[q % 2][:, g, :], gain_lo[q % 2][:, g, :], start=True, stop=True)
                ins.then_inc(b_made, 1)

            def state_inputs(j, q):
                pe.wait_ge(b_low, j + 1)
                wait(pe, state_ready, 4 * (j - 1))
                for g in range(GH):
                    k = q % 2 * 2 + g
                    pe.wait_ge(u_low, GH * j + g + 1)
                    o = v_ps[q % 2][:, g, 0:7 * B]
                    three(o, b_hi[:, g, P:2 * P], b_lo[:, g, P:2 * P], u_hi[k][:, 0, 0:7 * B], u_lo[k][:, 0, 0:7 * B],
                          start=g == 0, stop=False, skip=g == 1)
                    ins = three(o, b_hi[:, g, 0:P], b_lo[:, g, 0:P], u_hi[k][:, 1, 0:7 * B],
                                u_lo[k][:, 1, 0:7 * B], start=False, stop=True, skip=g == 1)
                ins.then_inc(v_done, 1)

            def carry(k, j, q):
                if k == 0:
                    pe.wait_ge(r_ready, 2 * GH * j + 2 * GH)
                    pe.wait_ge(state_first, j + 1)
                else:
                    pe.wait_ge(state_ready, 4 * j + k)
                dst, src, n = ((4, 4, 3), (5, 1, 1), (6, 2, 1), (1, 1, 3))[k]
                step = r2_sb if k in (1, 2) else r_sb
                for g in range(GH):
                    ins = pe.matmul(v_ps[q % 2][:, g, dst * B:(dst + n) * B], step[q % 2][:, g, :],
                                    s32[q % 2][:, g, src * B:(src + n) * B], start=False, stop=True,
                                    skip_group_check=True)
                ins.then_inc(state_added, 1)

            def local(i, j, q, g, a):
                k = q % 2 * 2 + g
                if a == 0:
                    wait(pe, y_masked, GH * j + g - 3)
                    if g == 0:
                        pe.wait_ge(toep_loaded[q], 16 * i + 16)
                y, t = y_ps[k], toep[q]
                o, cols = a * SUP, slice(a * P, (a + 1) * P)
                three(y[:, o:o + SUP], u_hi[k][:, 0, cols], u_lo[k][:, 0, cols], t[:, g, 0, :], t[:, g, 1, :],
                      start=a == 0, stop=False, skip=True)
                ins = three(y[:, o + T:o + SUP], u_hi[k][:, 1, cols], u_lo[k][:, 1, cols], t[:, g, 0, 0:T],
                            t[:, g, 1, 0:T], start=False, stop=False, skip=True)
                if a == 1:
                    ins.then_inc(y_local, 1)

            def from_state(j, q, g):
                if g == 0:
                    pe.wait_ge(s_low, j + 1)
                for a in range(2):
                    cols = slice(a * P, (a + 1) * P)
                    ins = three(y_ps[q % 2 * 2 + g][:, a * SUP:(a + 1) * SUP], s_hi[q % 2][:, g, cols],
                                s_lo[q % 2][:, g, cols], e_hi[q % 4][:, g, :], e_lo[q % 4][:, g, :],
                                start=False, stop=True, skip=True)
                ins.then_inc(y_done, 1)

            pe.wait_ge(tables_ready, 1)
            pe.wait_ge(gelu_done, 2 * B * NBLK)
            pe.wait_ge(mid_masked, B * NBLK)
            keep_clock(bank[7][:, :], g_hi[0][:, 0, :], 24)
            input_matrices(0, 0)
            for g in range(GH):
                turn(0, g, g)
            state_inputs(0, 0)

            def pairs_pe(i, first, last):
                for q in range(PPI):
                    j = i * PPI + q
                    start, end = first and q == 0, last and q == PPI - 1
                    nq = (q + 1) % PPI
                    ni = i + 1 if nq == 0 else i
                    carry(0, j, q)
                    if not end:
                        turn(ni, GH * (j + 1), GH * nq)
                    local(i, j, q, 0, 0)
                    carry(1, j, q)
                    local(i, j, q, 0, 1)
                    if not end:
                        input_matrices(j + 1, nq)
                    carry(2, j, q)
                    if not end:
                        turn(ni, GH * (j + 1) + 1, GH * nq + 1)
                    if not start:
                        from_state(j - 1, q + 3, 0)
                    carry(3, j, q)
                    local(i, j, q, 1, 0)
                    if not end:
                        state_inputs(j + 1, q + 1)
                    if not start:
                        from_state(j - 1, q + 3, 1)
                    local(i, j, q, 1, 1)
            peeled(pe, NI2, pairs_pe)
            for g in range(GH):
                from_state(CH // GH - 1, PPI - 1, g)


_INS = ["x", "itok_B_0_7", "itok_B_2182_4065", "itok_B_78_3631", "_lenS", "L0_cond_W_sess", "L0_cond_b_sess",
        "L0_cond_W2", "L0_cond_b2", "L1_cond_log_dt", "L1_cond_C", "L1_cond_log_A_real", "L1_cond_A_imag",
        "L1_cond_D"]


def kernel(**inputs):
    import numpy as _np
    import concourse.bacc as _bacc
    from concourse import mybir as _mybir
    from concourse.bass_utils import run_bass_kernel_spmd as _run

    nc = _bacc.Bacc("TRN2", target_bir_lowering=False, num_devices=1)
    arrays, args = {}, []
    for name in _INS:
        a = _np.ascontiguousarray(inputs[name])
        arrays[f"in_{name}_dram"] = a
        args.append(nc.dram_tensor(f"in_{name}_dram", a.shape, _mybir.dt.from_np(a.dtype), kind="ExternalInput").ap())
    out = nc.dram_tensor("out_dram", (B, CH, L), _mybir.dt.float32, kind="ExternalOutput").ap()
    session_and_state_space_layer(nc, *args, out)
    r = _run(nc, [arrays], core_ids=[0])
    return r.results[0]["out_dram"]
```
